# Optimizing a Trainium2 kernel written in Bass

```python
import numpy as np
import jax
import jax.numpy as jnp

def _softmax(x, axis=-1):
    return jax.nn.softmax(x, axis=axis)

def _gelu(x):
    return jax.nn.gelu(x, approximate=True)

def _silu(x):
    return jax.nn.silu(x)

def _sigmoid(x):
    return jax.nn.sigmoid(x)

def _layernorm(x, axis=-1, eps=1e-05):
    m = jnp.mean(x, axis=axis, keepdims=True)
    v = jnp.var(x, axis=axis, keepdims=True)
    return (x - m) / jnp.sqrt(v + eps)

def _scatter_add(tgt, idx, src, axis=0):
    return tgt.at[idx].add(src)

def _segment_sum(src, seg, n):
    return jax.ops.segment_sum(src, seg, n)
kernel_name = 'mk_xattn_ffn_d1_seqx_r8_af38a8'

def setup_inputs(seed: int=0):
    np.random.seed(seed)
    _w = jnp.asarray

    def _rec_inputs():
        import jax
        import jax.numpy as jnp
        _rk = jax.random.key(seed)
        x = -0.0005207 + 1.001 * jax.random.normal(jax.random.fold_in(_rk, 1), (16, 256, 128), jnp.float32)
        _lenS = 256 - jax.random.randint(jax.random.fold_in(_rk, 7), (16,), 0, max(1, 256 // 4) + 1, jnp.int32)
        _lenS2 = 1601 - jax.random.randint(jax.random.fold_in(_rk, 8), (16,), 0, max(1, 1601 // 4) + 1, jnp.int32)
        _ctx_1024P = jax.random.normal(jax.random.fold_in(_rk, 11), (16, 16, 128), jnp.float32)
        _ctx_1024c = jax.random.dirichlet(jax.random.fold_in(_rk, 511), 0.3 * jnp.ones((16,), jnp.float32), (16, 1601))
        _ctx_1024t = jnp.einsum('bsk,bkd->bsd', _ctx_1024c, _ctx_1024P)
        _ctx_1024t = _ctx_1024t * jax.lax.rsqrt(jnp.mean(jnp.square(_ctx_1024t)) + 1e-12) * 0.953939
        ctx_1024 = -0.000514642 + 1.00011 * (_ctx_1024t + 0.3 * jax.random.normal(jax.random.fold_in(_rk, 611), (16, 1601, 128), jnp.float32))
        return (x, ctx_1024)
    x, ctx_1024 = _rec_inputs()

    def _L0_xattn_setup():
        import jax, jax.numpy as jnp
        import numpy as np
        EMBED_DIM = 128
        NUM_HEADS = 16
        HEAD_DIM = EMBED_DIM // NUM_HEADS
        WINDOW = 64

        def apply_rope(x):
            B, H, S, d = x.shape
            half = d // 2
            pos = jnp.arange(S, dtype=x.dtype)
            freqs = 1.0 / 10000.0 ** (jnp.arange(half, dtype=x.dtype) / half)
            ang = pos[:, None] * freqs[None, :]
            cos, sin = (jnp.cos(ang), jnp.sin(ang))
            x1, x2 = (x[..., :half], x[..., half:])
            return jnp.concatenate([x1 * cos - x2 * sin, x1 * sin + x2 * cos], axis=-1)

        def _forward(query, key, value, q_w, q_b, k_w, k_b, v_w, v_b, o_w, o_b):
            B, S_q, D = query.shape
            S_k = key.shape[1]
            H, d, W = (NUM_HEADS, HEAD_DIM, WINDOW)
            q = (query @ q_w.T + q_b).reshape(B, S_q, H, d).transpose(0, 2, 1, 3)
            k = (key @ k_w.T + k_b).reshape(B, S_k, H, d).transpose(0, 2, 1, 3)
            v = (value @ v_w.T + v_b).reshape(B, S_k, H, d).transpose(0, 2, 1, 3)
            q = apply_rope(q) * d ** (-0.5)
            k = apply_rope(k)
            q_pos = jnp.arange(S_q)[:, None]
            offsets = jnp.arange(-W, 1)[None, :]
            idx = q_pos + offsets
            local_mask = (idx < 0) | (idx >= S_k)
            gidx = jnp.clip(idx, 0, S_k - 1)
            k_win = k[:, :, gidx, :]
            v_win = v[:, :, gidx, :]
            scores = jnp.einsum('bhqd,bhqwd->bhqw', q, k_win)
            mask = local_mask[None, None, :, :]
            scores = jnp.where(mask, -jnp.inf, scores)
            m = jnp.max(scores, axis=-1, keepdims=True)
            m = jnp.where(jnp.isfinite(m), m, 0.0)
            e = jnp.exp(scores - m)
            denom = jnp.sum(e, axis=-1, keepdims=True)
            probs = jnp.where(denom > 0, e / jnp.where(denom > 0, denom, 1.0), 0.0)
            ctx = jnp.einsum('bhqw,bhqwd->bhqd', probs, v_win)
            ctx = ctx.transpose(0, 2, 1, 3).reshape(B, S_q, D)
            return ctx @ o_w.T + o_b
        key = jax.random.key(seed)
        ks = jax.random.split(key, 12)
        B, S, D = (1, 256, EMBED_DIM)
        scale = 1.0 / np.sqrt(D)
        inp = {'query': jax.random.normal(ks[0], (B, S, D), jnp.float32), 'key': jax.random.normal(ks[1], (B, S, D), jnp.float32), 'value': jax.random.normal(ks[2], (B, S, D), jnp.float32), 'q_w': jax.random.normal(ks[3], (D, D), jnp.float32) * scale, 'q_b': jax.random.normal(ks[4], (D,), jnp.float32) * 0.01, 'k_w': jax.random.normal(ks[5], (D, D), jnp.float32) * scale, 'k_b': jax.random.normal(ks[6], (D,), jnp.float32) * 0.01, 'v_w': jax.random.normal(ks[7], (D, D), jnp.float32) * scale, 'v_b': jax.random.normal(ks[8], (D,), jnp.float32) * 0.01, 'o_w': jax.random.normal(ks[9], (D, D), jnp.float32) * scale, 'o_b': jax.random.normal(ks[10], (D,), jnp.float32) * 0.01}
        return inp
    _L0_xattn_all = _L0_xattn_setup()
    _L0_xattn_in = {k: v for k, v in _L0_xattn_all.items() if k in ('q_w', 'q_b', 'k_w', 'k_b', 'v_w', 'v_b', 'o_w', 'o_b')}
    del _L0_xattn_all

    def _L0_ffn_setup():
        import jax, jax.numpy as jnp
        import numpy as np
        NUM_EXPERTS = 8
        TOP_K = 2
        CAP_RATIO = 1.25
        INIT_STD = 0.02
        key = jax.random.key(seed)
        k1, k2, k3, k4 = jax.random.split(key, 4)
        B, T, H, F = (4, 256, 128, 512)
        x = jax.random.normal(k1, (B, T, H), jnp.float32)
        router_w = jax.random.normal(k2, (NUM_EXPERTS, H), jnp.float32) * INIT_STD
        w1 = jax.random.normal(k3, (NUM_EXPERTS, H, F), jnp.float32) * INIT_STD
        w2 = jax.random.normal(k4, (NUM_EXPERTS, F, H), jnp.float32) * INIT_STD
        return {'x': x, 'router_w': router_w, 'w1': w1, 'w2': w2}
    _L0_ffn_all = _L0_ffn_setup()
    _L0_ffn_in = {k: v for k, v in _L0_ffn_all.items() if k in ('router_w', 'w1', 'w2')}
    del _L0_ffn_all
    return {'x': x, 'ctx_1024': ctx_1024, 'L0_xattn_q_w': _L0_xattn_in['q_w'], 'L0_xattn_q_b': _L0_xattn_in['q_b'], 'L0_xattn_k_w': _L0_xattn_in['k_w'], 'L0_xattn_k_b': _L0_xattn_in['k_b'], 'L0_xattn_v_w': _L0_xattn_in['v_w'], 'L0_xattn_v_b': _L0_xattn_in['v_b'], 'L0_xattn_o_w': _L0_xattn_in['o_w'], 'L0_xattn_o_b': _L0_xattn_in['o_b'], 'L0_ffn_router_w': _L0_ffn_in['router_w'], 'L0_ffn_w1': _L0_ffn_in['w1'], 'L0_ffn_w2': _L0_ffn_in['w2']}

def reference(x, ctx_1024, L0_xattn_q_w, L0_xattn_q_b, L0_xattn_k_w, L0_xattn_k_b, L0_xattn_v_w, L0_xattn_v_b, L0_xattn_o_w, L0_xattn_o_b, L0_ffn_router_w, L0_ffn_w1, L0_ffn_w2):
    import jax
    import jax.numpy as jnp

    def _L0_xattn_ref(query, key, value, q_w, q_b, k_w, k_b, v_w, v_b, o_w, o_b):
        import jax, jax.numpy as jnp
        import numpy as np
        EMBED_DIM = 128
        NUM_HEADS = 16
        HEAD_DIM = EMBED_DIM // NUM_HEADS
        WINDOW = 64

        def apply_rope(x):
            B, H, S, d = x.shape
            half = d // 2
            pos = jnp.arange(S, dtype=x.dtype)
            freqs = 1.0 / 10000.0 ** (jnp.arange(half, dtype=x.dtype) / half)
            ang = pos[:, None] * freqs[None, :]
            cos, sin = (jnp.cos(ang), jnp.sin(ang))
            x1, x2 = (x[..., :half], x[..., half:])
            return jnp.concatenate([x1 * cos - x2 * sin, x1 * sin + x2 * cos], axis=-1)

        def _forward(query, key, value, q_w, q_b, k_w, k_b, v_w, v_b, o_w, o_b):
            B, S_q, D = query.shape
            S_k = key.shape[1]
            H, d, W = (NUM_HEADS, HEAD_DIM, WINDOW)
            q = (query @ q_w.T + q_b).reshape(B, S_q, H, d).transpose(0, 2, 1, 3)
            k = (key @ k_w.T + k_b).reshape(B, S_k, H, d).transpose(0, 2, 1, 3)
            v = (value @ v_w.T + v_b).reshape(B, S_k, H, d).transpose(0, 2, 1, 3)
            q = apply_rope(q) * d ** (-0.5)
            k = apply_rope(k)
            q_pos = jnp.arange(S_q)[:, None]
            offsets = jnp.arange(-W, 1)[None, :]
            idx = q_pos + offsets
            local_mask = (idx < 0) | (idx >= S_k)
            gidx = jnp.clip(idx, 0, S_k - 1)
            k_win = k[:, :, gidx, :]
            v_win = v[:, :, gidx, :]
            scores = jnp.einsum('bhqd,bhqwd->bhqw', q, k_win)
            mask = local_mask[None, None, :, :]
            scores = jnp.where(mask, -jnp.inf, scores)
            m = jnp.max(scores, axis=-1, keepdims=True)
            m = jnp.where(jnp.isfinite(m), m, 0.0)
            e = jnp.exp(scores - m)
            denom = jnp.sum(e, axis=-1, keepdims=True)
            probs = jnp.where(denom > 0, e / jnp.where(denom > 0, denom, 1.0), 0.0)
            ctx = jnp.einsum('bhqw,bhqwd->bhqd', probs, v_win)
            ctx = ctx.transpose(0, 2, 1, 3).reshape(B, S_q, D)
            return ctx @ o_w.T + o_b
        return _forward(query, key, value, q_w, q_b, k_w, k_b, v_w, v_b, o_w, o_b)

    def _L0_ffn_ref(x, router_w, w1, w2):
        import jax, jax.numpy as jnp
        import numpy as np
        NUM_EXPERTS = 8
        TOP_K = 2
        CAP_RATIO = 1.25
        INIT_STD = 0.02
        B, T, H = x.shape
        E, K = (NUM_EXPERTS, TOP_K)
        xf = x.reshape(-1, H)
        N = xf.shape[0]
        P = N * K
        capacity = int(CAP_RATio * N * K / E) + 1 if False else int(CAP_RATIO * N * K / E) + 1
        logits = xf @ router_w.T
        probs = jax.nn.softmax(logits, axis=-1)
        k_probs, k_idx = jax.lax.top_k(probs, K)
        k_probs = k_probs / jnp.sum(k_probs, axis=-1, keepdims=True)
        flat_e = k_idx.reshape(-1)
        onehot = jax.nn.one_hot(flat_e, E, dtype=jnp.int32)
        rank = jnp.take_along_axis(jnp.cumsum(onehot, axis=0) - 1, flat_e[:, None], axis=1)[:, 0]
        keep = rank < capacity
        slot = jnp.minimum(rank, capacity - 1)
        token_id = jnp.arange(P) // K
        dispatched = jnp.where(keep[:, None], xf[token_id], 0.0)
        buf = jnp.zeros((E, capacity, H), x.dtype).at[flat_e, slot].add(dispatched)
        h = jax.nn.silu(jnp.einsum('ech,ehf->ecf', buf, w1))
        out_buf = jnp.einsum('ecf,efh->ech', h, w2)
        pair_out = out_buf[flat_e, slot] * keep[:, None].astype(x.dtype)
        combined = jnp.sum(pair_out.reshape(N, K, H) * k_probs[..., None], axis=1)
        return combined.reshape(B, T, H) + x
    x = x + _L0_xattn_ref(_layernorm(x, axis=-1), ctx_1024, ctx_1024, L0_xattn_q_w, L0_xattn_q_b, L0_xattn_k_w, L0_xattn_k_b, L0_xattn_v_w, L0_xattn_v_b, L0_xattn_o_w, L0_xattn_o_b)
    x = x + _L0_ffn_ref(_layernorm(x, axis=-1), L0_ffn_router_w, L0_ffn_w1, L0_ffn_w2)
    return x

_drawn_inputs = setup_inputs


def setup_inputs(seed=0):
    import zlib

    import numpy as np

    out = dict(_drawn_inputs(seed))
    spreads = {}
    factors = {'L0_xattn_q_b': 8.0,
     'L0_xattn_k_b': 22.97,
     'L0_xattn_v_b': 5.681,
     'L0_xattn_o_b': 5.68,
     'L0_ffn_router_w': 3.761,
     'L0_ffn_w1': 3.331,
     'L0_ffn_w2': 3.338}
    for name, (base, spread) in spreads.items():
        noise = np.random.default_rng([zlib.crc32(name.encode()), seed]).standard_normal(out[name].shape)
        drawn = base * np.exp(spread * noise) if base else spread * noise
        out[name] = jnp.asarray(drawn.astype(out[name].dtype))
    for name, factor in factors.items():
        out[name] = (out[name] * factor).astype(out[name].dtype)
    return out
```

```python
from contextlib import ExitStack

import numpy as np

import concourse.bass as bass
from concourse import mybir

F32 = mybir.dt.float32
F32R = mybir.dt.float32r
BF16 = mybir.dt.bfloat16
I32 = mybir.dt.int32
ALU = mybir.AluOpType
ACT = mybir.ActivationFunctionType
AX = mybir.AxisListType.X

P = 128
BATCHES = 16
TOKENS = 256
CONTEXT = 1601
DIM = 128
HEADS = 16
HD = DIM // HEADS
BLOCK = 64
TILES = TOKENS // P
GROUPS = HEADS // 4
UNITS = GROUPS * TILES
EXPERTS = 8
HIDDEN = 512
ALL = BATCHES * TOKENS
CAPACITY = int(1.25 * ALL * 2 / EXPERTS) + 1
QUEUE = 1344
INIT_P = 64
INIT_R = QUEUE // INIT_P
USED = 1284
ROW = DIM + 2
EPS = 1e-5
MASKED = -1e30
FAR = float(1 << 20)
PARTS = 3
PAIRS = 6
FLAG_ROW = PAIRS * HD
MAX_ROWS = FLAG_ROW + 1
CONST_ROWS = P - FLAG_ROW
KEY_TILE = [0, 0, 1, 2]

CHUNKS = [512, 512, USED - 1024]
FC = HIDDEN // P

IDENT, COSQ, SINQ, COSK, SINK = 0, P, P + TOKENS, P + 2 * TOKENS, P + 3 * TOKENS
DESC8 = P + 4 * TOKENS
LIMIT = DESC8 + 16
START = LIMIT + 8
TOK = START + 8
CONSTS = TOK + 2
WQ, WQR, WK, WKR, WV, WO, WR = (n * DIM for n in range(7))
WEIGHTS = WR + EXPERTS


def build(nc, x, ctx_in, weights, col_bias, row_bias, consts, consts16, q_rows, k_rows, w1, w2, out):
    scr = nc.dram_tensor("parts_scratch", [BATCHES, 2, PARTS, P, TOKENS], BF16).ap()
    scr_m = nc.dram_tensor("maxima_scratch", [2, 2, 2, 16 * P], BF16).ap()
    queues = nc.dram_tensor("queues", [EXPERTS * QUEUE, ROW], F32).ap()

    es = ExitStack()
    with es:
        def sb(name, shape, dt=F32):
            return es.enter_context(nc.sbuf_tensor(name, shape, dt))

        def two(name, shape, dt=F32):
            return [sb(f"{name}{n}", shape, dt) for n in range(2)]

        def sem(name):
            return es.enter_context(nc.semaphore(name))

        bank = [es.enter_context(nc.psum_tensor(f"bank{n}", [P, 512], F32)) for n in range(8)]

        cst = sb("cst", [P, CONSTS])
        cst16 = sb("cst16", [P, 3 * P], BF16)
        wts = sb("wts", [P, WEIGHTS])
        cbias = sb("cbias", [P, 4])
        rbias = sb("rbias", [P, 2, DIM])
        ident = cst[:, IDENT:IDENT + P]
        ident16, earlier16, ones16 = (cst16[:, n * P:(n + 1) * P] for n in range(3))
        count = sb("count", [P, EXPERTS])
        tok = sb("tok", [P, TILES])
        half_neg = sb("half_neg", [P, TILES])

        xin = two("xin", [P, TILES, DIM])
        cin = two("cin", [P, TILES, DIM])
        xn1 = two("xn1", [P, TILES, DIM])
        stats1 = sb("stats1", [P, TILES, 6])
        mv1 = sb("mv1", [P, TILES, 2])
        var1 = sb("var1", [P, TILES])
        rstd1 = sb("rstd1", [P, TILES])
        xcT = two("xcT", [P, 2 * TOKENS])
        straight = sb("straight", [P, 2, TOKENS])
        turned = sb("turned", [P, 2, TOKENS])
        qk = sb("qk", [P, 2, TOKENS])
        rest = sb("rest", [P, 2, TOKENS])
        parts = sb("parts", [P, PARTS, 2, TOKENS], BF16)
        v_sb = two("v_sb", [P, 3, HEADS, 32])
        maxima = two("maxima", [P, HEADS, TILES])
        max_parts = two("max_parts", [P, 2, 8, TILES], BF16)
        maxT = two("maxT", [2 * 8 * TILES, P], BF16)
        probs = two("probs", [P, 512])
        csb = two("csb", [P, GROUPS, TOKENS])
        recip = two("recip", [P, HEADS])
        ctxn = sb("ctxn", [P, TILES, DIM])
        ctxT = sb("ctxT", [P, TOKENS])
        xres = two("xres", [P, TILES, DIM])
        x1 = two("x1", [P, TILES, DIM])
        stats2 = sb("stats2", [P, TILES, 6])
        mv2 = sb("mv2", [P, TILES, 2])
        var2 = sb("var2", [P, TILES])
        rstd2 = sb("rstd2", [P, TILES])
        rows = two("rows", [P, 2, TILES, ROW])
        base = two("base", [P, TILES, DIM])
        xn2T = sb("xn2T", [P, TOKENS])
        top = sb("top", [P, 2, TILES])
        diff = sb("diff", [P, TILES])
        ediff = sb("ediff", [P, TILES])
        gate = sb("gate", [P, 2, TILES])
        eq = sb("eq", [P, TILES, EXPERTS])
        weighed = sb("weighed", [P, TILES, EXPERTS])
        best = sb("best", [P, 2, TILES])
        logits2 = sb("logits2", [P, TILES, EXPERTS])
        chosen = sb("chosen", [P, 2, TILES, EXPERTS])
        both16 = sb("both16", [P, TILES, EXPERTS], BF16)
        place = sb("place", [P, TILES, EXPERTS])
        over = sb("over", [P, TILES, EXPERTS])
        place2 = sb("place2", [P, TILES, EXPERTS])
        picked = sb("picked", [P, 2, TILES, EXPERTS])
        index = two("index", [P, 2 * TILES], I32)
        empty = sb("empty", [INIT_P, INIT_R, ROW])

        xs = two("xs", [P, 11, ROW])
        w1raw = two("w1raw", [P, HIDDEN])
        w2raw = two("w2raw", [P, FC, DIM])
        w1p = two("w1p", [P, 2, HIDDEN], F32R)
        w2p = two("w2p", [P, 2, FC, DIM], F32R)
        xTp = two("xTp", [P, 2, 512], F32R)
        yT = two("yT", [P, 512])
        ys = two("ys", [P, 4, DIM])
        with ExitStack() as packs:
            def pack_buffers(name, shape):
                return [packs.enter_context(nc.sbuf_tensor(f"{name}{n}", shape, BF16)) for n in range(2)]

            q_pack = pack_buffers("q_pack", [P, HEADS, TOKENS])
            k_pack = pack_buffers("k_pack", [P, 2, HEADS, TOKENS])
        hid = two("hid", [P, FC, 512])
        hidp = two("hidp", [P, 2, FC, 512], F32R)

        S = {}
        for name in """consts_in x_in c_in init_made init_out dump_out v_ones counted half_set
            stats1_s mv1_s var1_s rstd1_s xn1_s xt_mm xct_s q_mm k_mm roped_q roped_k qk_s part1 rest_s part2 part3
            scr_w packed0 packed1 a_mm max_s mparts mt_mm mt_s mscr_w m_packed0 m_packed1 v_mm v_s b_mm prob_s pv_mm csb_s
            ct_mm rec_s norm_s ctxt_mm ctxt_s y_mm xr_in xrb_s x1_s stats2_s mv2_s var2_s rstd2_s xn2_s
            rowcopy_s base_s tok_s base_out0 base_out1 xn2t_mm xn2t_s logit_mm top_s exp_gate gate_s both_s prefix_mm ranked
            router router_psum past_dve past_pool past_sp scattered0 scattered1
            xs_in w_in w_hi w_lo xt2_mm xt_hi xt_lo up_mm silu_s h_hi h_lo down_mm yt_s yt_mm ys_s added0 added1 added2""".split():
            S[name] = sem(name)

        block = es.enter_context(nc.Block())

        def after(eng, name, per, batch, n=None):
            n = per if n is None else n
            if isinstance(batch, int):
                if batch >= BATCHES:
                    batch, n = BATCHES - 1, per
                if batch * per + n <= 0:
                    return
            eng.wait_ge(S[name], batch * per + n)

        def after_same(eng, name, per, par, pair, ahead):
            n = pair + (par + ahead) // 2
            if not isinstance(n, int) or n >= 0:
                eng.wait_ge(S[f"{name}{(par + ahead) % 2}"], n * per + per)

        CONST_LOADS = 11 * 16

        def apart(eng, name):
            eng.sem_inc(S[name], 1)

        def on(batch):
            return not isinstance(batch, int) or 0 <= batch < BATCHES

        FIRST, LOOP, END, LAST = -4, 2, 12, 18

        def steps(eng, body):
            for k in range(FIRST, LOOP):
                body(k, k % 2, k // 2)
            with eng.Fori(0, (END - LOOP) // 2) as n:
                body(n * 2 + LOOP, 0, n + LOOP // 2)
                body(n * 2 + (LOOP + 1), 1, n + LOOP // 2)
            for k in range(END, LAST):
                body(k, k % 2, k // 2)

        EX_LOOP, EX_END = 1, 7

        def experts(eng, body):
            body(0, 0)
            with eng.Fori(0, (EX_END - EX_LOOP) // 2) as n:
                body(n * 2 + EX_LOOP, 1)
                body(n * 2 + (EX_LOOP + 1), 0)
            body(7, 1)

        NCH = len(CHUNKS)

        def chunk_done(eng, name, per, e, c, n=None):
            n = per if n is None else n
            v = (e * NCH + c) * per + n
            if isinstance(e, int) and v <= 0:
                return
            eng.wait_ge(S[name], v)

        def added_all(eng, e):
            for c in range(NCH):
                eng.wait_ge(S[f"added{c}"], e * (16 * len(tiles_of(c))))

        def tiles_of(c):
            return [(4 * c + t, t * P, min(P, CHUNKS[c] - t * P)) for t in range(-(-CHUNKS[c] // P))]

        @block.sync
        def _(sp):
            def load_x(j, par):
                if not on(j):
                    return
                after(sp, "xn1_s", 2, j - 2)
                apart(sp, "past_sp")
                after(sp, "stats1_s", 2, j - 1)
                apart(sp, "past_sp")
                sp.dma_start(xin[par][:], x[j, :, :].rearrange("(t p) c -> p t c", p=P)).then_inc(S["x_in"], 16)

            def load_context(j, par):
                if not on(j):
                    return
                after(sp, "xt_mm", 1, j - 1)
                apart(sp, "past_sp")
                sp.dma_start(cin[par][:], ctx_in[j, 0:TOKENS, :].rearrange("(t p) c -> p t c", p=P)).then_inc(S["c_in"], 16)

            load_x(0, 0)
            load_context(0, 0)
            sp.dma_start(cst[:], consts).then_inc(S["consts_in"], 16)
            sp.dma_start(wts[:], weights).then_inc(S["consts_in"], 16)
            sp.dma_start(cst16[:], consts16).then_inc(S["consts_in"], 16)
            sp.dma_start(cbias[:], col_bias).then_inc(S["consts_in"], 16)
            sp.dma_start(rbias[:], row_bias.unsqueeze(0).to_broadcast([P, 2, DIM])).then_inc(S["consts_in"], 16)
            for n in range(2):
                sp.dma_start(q_pack[n][FLAG_ROW:P, :, :],
                             q_rows.unsqueeze(1).to_broadcast([CONST_ROWS, HEADS, TOKENS])).then_inc(S["consts_in"], 16)
                for v in range(2):
                    sp.dma_start(k_pack[n][FLAG_ROW:P, v, :, :],
                                 k_rows[:, v, :].unsqueeze(1).to_broadcast([CONST_ROWS, HEADS, TOKENS])
                                 ).then_inc(S["consts_in"], 16)

            def pack(j, par, half):
                if not on(j):
                    return
                after(sp, "scr_w", 32, j)
                apart(sp, "past_sp")
                after(sp, "b_mm", UNITS, j - 2, 4 * half + 4)
                hs = slice(8 * half, 8 * half + 8)
                cs = slice(8 * half * TOKENS, (8 * half + 8) * TOKENS)
                src = scr[j].rearrange("s n (d h) t -> s n d (h t)", d=HD)
                r0 = 0
                for part, times in ((0, 3), (1, 2), (2, 1)):
                    s = src[0, part, :, cs]
                    if times > 1:
                        s = s.unsqueeze(0).to_broadcast([times, HD, 8 * TOKENS])
                    sp.dma_start(q_pack[par][r0:r0 + times * HD, hs, :].rearrange("p h t -> p (h t)"), s
                                 ).then_inc(S[f"packed{half}"], 16)
                    r0 += times * HD
                sp.dma_start(q_pack[par][MAX_ROWS:MAX_ROWS + 2, hs, :],
                             q_rows[1:3, :].unsqueeze(1).to_broadcast([2, 8, TOKENS])).then_inc(S[f"packed{half}"], 16)
                for v in range(2):
                    r0 = 0
                    for run in (3, 2, 1):
                        sp.dma_start(k_pack[par][r0:r0 + run * HD, v, hs, :].rearrange("p h t -> p (h t)"),
                                     src[1, 0:run, :, cs].rearrange("n d f -> (n d) f")).then_inc(S[f"packed{half}"], 16)
                        r0 += run * HD

            def pack_maxima(j, par, half):
                if not on(j):
                    return
                after(sp, "mt_s", 2, j, half + 1)
                apart(sp, "past_sp")
                after(sp, f"m_packed{half}", 16, j - 2)
                sp.dma_start(scr_m[par, half].rearrange("s (r q) -> (s r) q", q=P), maxT[half][:]).then_inc(S["mscr_w"], 16)
                after(sp, "mscr_w", 32, j, 16 * half + 16)
                sp.dma_start(q_pack[par][MAX_ROWS:MAX_ROWS + 2, 8 * half:8 * half + 8, :].rearrange("p h t -> p (h t)"),
                             scr_m[par, half]).then_inc(S[f"m_packed{half}"], 16)

            def body(k, par, pair):
                if not (isinstance(k, int) and k == FIRST):
                    load_x(k + 4, par)
                if on(k - 1):
                    after(sp, "x1_s", 1, k - 3)
                    apart(sp, "past_sp")
                    after(sp, "xrb_s", 1, k - 2)
                    sp.dma_start(xres[1 - par][:], x[k - 1, :, :].rearrange("(t p) c -> p t c", p=P)).then_inc(S["xr_in"], 16)
                pack_maxima(k, par, 1)
                if on(k + 2):
                    after(sp, "part3", 1, k + 2)
                    for s in range(2):
                        sp.dma_start(scr[k + 2, s].rearrange("n p t -> p n t"), parts[:, :, s, :]).then_inc(S["scr_w"], 16)
                if on(k - 2):
                    after(sp, "base_s", 1, k - 2)
                    sp.dma_start(out[bass.ds((k - 2) * TOKENS, TOKENS), :].rearrange("(t p) c -> p t c", p=P),
                                 base[par][:]).then_inc(S[f"base_out{par}"], 16)
                if not (isinstance(k, int) and k == FIRST):
                    load_context(k + 4, par)
                pack(k + 2, par, 0)
                pack_maxima(k + 1, 1 - par, 0)
                pack(k + 2, par, 1)
            steps(sp, body)

            def load_expert(e, par):
                if isinstance(e, int) and e >= EXPERTS:
                    return
                chunk_done(sp, "ys_s", 1, e - 2, NCH - 1)
                apart(sp, "past_sp")
                chunk_done(sp, "xt2_mm", 1, e - 1, 0)
                apart(sp, "past_sp")
                if not isinstance(e, int) or e >= 2:
                    for c in range(NCH):
                        sp.wait_ge(S[f"added{c}"], (e - 1) * (16 * len(tiles_of(c))))
                        apart(sp, "past_sp")
                start = e * QUEUE
                sp.dma_start(xs[par][:, 0:10, :],
                             queues[bass.ds(start, 10 * P), :].rearrange("(p t) c -> p t c", t=10)).then_inc(S["xs_in"], 16)
                sp.dma_start(xs[par][0:USED - 10 * P, 10, :],
                             queues[bass.ds(start + 10 * P, USED - 10 * P), :]).then_inc(S["xs_in"], 16)

            def load_weights(e, par):
                if isinstance(e, int) and e >= EXPERTS:
                    return
                if not isinstance(e, int) or e >= 2:
                    sp.wait_ge(S["w_lo"], (e - 1) * 2)
                    apart(sp, "past_sp")
                if not isinstance(e, int) or e >= 1:
                    sp.wait_ge(S["w_hi"], e * 2)
                    apart(sp, "past_sp")
                sp.dma_start(w1raw[par][:], w1[e, :, :]).then_inc(S["w_in"], 16)
                sp.dma_start(w2raw[par][:], w2[e, :, :].rearrange("(c f) h -> f c h", f=P)).then_inc(S["w_in"], 16)

            load_weights(0, 0)
            for n in range(2):
                sp.wait_ge(S[f"scattered{n}"], BATCHES // 2 * 2 * TILES * 16)
            load_expert(0, 0)

            def body2(e, par):
                load_weights(e + 1, 1 - par)
                load_expert(e + 1, 1 - par)
            experts(sp, body2)
            sp.wait_ge(S["init_out"], 16 * EXPERTS)
            sp.wait_ge(S["dump_out"], 16)
            for n in range(2):
                sp.wait_ge(S[f"base_out{n}"], 16 * BATCHES // 2)
            added_all(sp, EXPERTS)

        @block.tensor
        def _(pe):
            def mm(o, l, r, start=True, stop=True):
                return nc.tensor.matmul(o, l, r, start=start, stop=stop)

            ab, bb, cb = bank[0:2], bank[2:4], bank[4]
            m0, m1, m2 = bank[5:8]

            def m0_read(k, n):
                after(pe, "v_s", 1, k + 1 if n > 0 else k)
                after(pe, "norm_s", 2, k - 1 if n > 1 else k - 2, 1 if n > 1 else 2)
                after(pe, "roped_q", 2, k + 3 if n > 2 else k + 2)
                after(pe, "ranked", 1, k - 3)

            def m1_read(k, n):
                after(pe, "mt_s", 2, k if n > 0 else k, 2 if n > 0 else 1)
                after(pe, "xct_s", 1, k + 3 if n > 1 else k + 2)
                after(pe, "norm_s", 2, k - 1 if n > 2 else k - 2)
                after(pe, "mt_s", 2, k + 1 if n > 3 else k, 1)
                after(pe, "ctxt_s", 1, k - 2)

            def m2_read(k, n):
                after(pe, "xn2t_s", 1, k - 2 if n > 0 else k - 3)
                after(pe, "router_psum", 1, k - 2 if n > 1 else k - 3)
                after(pe, "roped_k", 2, k + 3 if n > 2 else k + 2)
                after(pe, "x1_s", 1, k - 2)

            def scores_by_query(j, par, u):
                if not on(j):
                    return
                hg, i2 = divmod(u, TILES)
                if u % 4 == 0:
                    after(pe, f"packed{u // 4}", 160, j)
                after(pe, "max_s", UNITS, j, u - 1)
                for hj in range(4):
                    for odd in range(2):
                        i, h = 2 * i2 + odd, 4 * hg + hj
                        ks = max(0, BLOCK * (i - 1))
                        last = mm(ab[u % 2][BLOCK * odd:BLOCK * odd + BLOCK, hj * P:(hj + 1) * P],
                                  q_pack[par][:, h, BLOCK * i:BLOCK * (i + 1)], k_pack[par][:, odd, h, ks:ks + P])
                last.then_inc(S["a_mm"], 1)

            def scores_by_key(j, par, u):
                if not on(j):
                    return
                hg, i2 = divmod(u, TILES)
                if u % 4 == 0:
                    after(pe, f"m_packed{u // 4}", 16, j)
                after(pe, "prob_s", UNITS, j, u - 1)
                for hj in range(4):
                    for odd in range(2):
                        i, h = 2 * i2 + odd, 4 * hg + hj
                        ks = max(0, BLOCK * (i - 1))
                        last = mm(bb[u % 2][:, hj * P + odd * BLOCK:hj * P + (odd + 1) * BLOCK],
                                  k_pack[par][:, odd, h, ks:ks + P], q_pack[par][:, h, BLOCK * i:BLOCK * (i + 1)])
                last.then_inc(S["b_mm"], 1)

            def weigh_values(j, par, u):
                if not on(j):
                    return
                hg, i2 = divmod(u, TILES)
                if u == 0:
                    after(pe, "v_s", 1, j)
                if u % 4 == 0:
                    after(pe, "csb_s", 2, j, u // 4)
                after(pe, "prob_s", UNITS, j, u + 1)
                for odd in range(2):
                    i = 2 * i2 + odd
                    for hj in range(4):
                        col = (hg % 2) * TOKENS + BLOCK * i
                        last = mm(cb[32 * hj:32 * hj + 32, col:col + BLOCK],
                                  v_sb[par][:, KEY_TILE[i], 4 * hg + hj, :],
                                  probs[u % 2][:, hj * P + odd * BLOCK:hj * P + (odd + 1) * BLOCK])
                last.then_inc(S["pv_mm"], 1)

            def values(k, par):
                j = k + 1
                if on(j):
                    m0_read(k, 0)
                    after(pe, "xct_s", 1, j)
                    for a in range(3):
                        last = mm(m0[:, a * P:(a + 1) * P], xcT[1 - par][:, TOKENS + BLOCK * a:TOKENS + BLOCK * a + P],
                                  wts[:, WV:WV + DIM])
                    last.then_inc(S["v_mm"], 1)

            def maxima_across(k, j, half, n):
                if on(j):
                    m1_read(k, n)
                    after(pe, "mparts", 4, j, 2 * half + 2)
                    nc.tensor.transpose(m1[0:32, 0:64].bitcast(BF16),
                                        max_parts[half][:].rearrange("p s h i -> p (s h i)"), ident16
                                        ).then_inc(S["mt_mm"], 1)

            def inputs_across(k, par):
                j = k + 3
                if on(j):
                    m1_read(k, 1)
                    after(pe, "xn1_s", 2, j)
                    after(pe, "c_in", 16, j)
                    for t in range(TILES):
                        nc.tensor.transpose(m1[:, t * P:(t + 1) * P], xn1[1 - par][:, t, :], ident)
                    for t in range(TILES):
                        last = nc.tensor.transpose(m1[:, (2 + t) * P:(3 + t) * P], cin[1 - par][:, t, :], ident)
                    last.then_inc(S["xt_mm"], 1)

            def project(k, par, m, w, wr, cols, name, free, n):
                if on(k + 3):
                    free(k, n)
                    after(pe, "xct_s", 1, k + 3)
                    mm(m[:, 0:TOKENS], wts[:, w:w + DIM], xcT[1 - par][:, cols:cols + TOKENS])
                    mm(m[:, TOKENS:2 * TOKENS], wts[:, wr:wr + DIM], xcT[1 - par][:, cols:cols + TOKENS]
                       ).then_inc(S[name], 1)

            def context_across(k, par, t):
                j = k - 1
                if on(j):
                    (m0_read if t == 0 else m1_read)(k, 1 + t)
                    after(pe, "csb_s", 2, j)
                    for g in range(GROUPS):
                        last = nc.tensor.transpose((m0, m1)[t][:, g * P:(g + 1) * P],
                                                   csb[1 - par][:, g, t * P:(t + 1) * P], ident)
                    last.then_inc(S["ct_mm"], 1)

            def body(k, par, pair):
                for u in range(UNITS):
                    scores_by_key(k, par, u)
                    scores_by_query(k + 1, 1 - par, u)
                    if u == 0:
                        values(k, par)
                        maxima_across(k, k, 1, 0)
                    if u == 1:
                        inputs_across(k, par)
                        if on(k - 2):
                            m2_read(k, 0)
                            after(pe, "xn2_s", 2, k - 2)
                            for t in range(TILES):
                                last = nc.tensor.transpose(m2[:, t * P:(t + 1) * P], rows[par][:, 0, t, 0:DIM], ident)
                            last.then_inc(S["xn2t_mm"], 1)
                    if u == 2:
                        context_across(k, par, 0)
                        if on(k - 2):
                            m2_read(k, 1)
                            for t in range(TILES):
                                last = mm(m2[:, t * EXPERTS:(t + 1) * EXPERTS], xn2T[:, t * P:(t + 1) * P],
                                          wts[:, WR:WR + EXPERTS])
                            last.then_inc(S["logit_mm"], 1)
                    if u == 3:
                        context_across(k, par, 1)
                        project(k, par, m0, WQ, WQR, 0, "q_mm", m0_read, 2)
                    if u == 4:
                        project(k, par, m2, WK, WKR, TOKENS, "k_mm", m2_read, 2)
                        maxima_across(k, k + 1, 0, 3)
                    if u == 5:
                        if on(k - 2):
                            m0_read(k, 3)
                            after(pe, "both_s", 1, k - 2)
                            b = both16[:].rearrange("p t e -> p (t e)")
                            mm(m0[:, 0:16], earlier16, b, True, False)
                            mm(m0[:, 8:16], ones16, b[:, 0:8], False, True)
                            mm(m0[:, 16:24], ones16, b[:, 0:8], True, False)
                            mm(m0[:, 16:24], ones16, b[:, 8:16], False, True).then_inc(S["prefix_mm"], 1)
                        if on(k - 1):
                            m1_read(k, 4)
                            after(pe, "norm_s", 2, k - 1)
                            for t in range(TILES):
                                last = nc.tensor.transpose(m1[:, t * P:(t + 1) * P], ctxn[:, t, :], ident)
                            last.then_inc(S["ctxt_mm"], 1)
                    if u == 6 and on(k - 1):
                        m2_read(k, 3)
                        after(pe, "ctxt_s", 1, k - 1)
                        for t in range(TILES):
                            last = mm(m2[:, t * P:(t + 1) * P], ctxT[:, t * P:(t + 1) * P], wts[:, WO:WO + DIM])
                        last.then_inc(S["y_mm"], 1)
                    if u == 0:
                        weigh_values(k - 1, 1 - par, UNITS - 1)
                    else:
                        weigh_values(k, par, u - 1)

            pe.wait_ge(S["consts_in"], CONST_LOADS)
            steps(pe, body)

            up, down, xt, yt = bank[0:4], bank[4], bank[5], bank[6]

            def rows_across(e, par, c):
                c0 = e * NCH + c
                if c == 0:
                    if isinstance(e, int) and e >= EXPERTS:
                        return
                    pe.wait_ge(S["xs_in"], e * 32 + 32)
                chunk_done(pe, "xt_hi", 1, e, c - 1)
                chunk_done(pe, "xt_lo", 1, e, c - 1)
                for t, col, n in tiles_of(c):
                    last = nc.tensor.transpose(xt[:, col:col + n], xs[par][0:n, t, 0:DIM], ident[0:n, 0:n])
                last.then_inc(S["xt2_mm"], 1)

            def hidden(e, par, c, sp_):
                n = CHUNKS[c]
                chunk_done(pe, "xt_lo", 1, e, c)
                if c == 0:
                    pe.wait_ge(S["w_lo"], 2 * e + 2)
                for f in range(FC):
                    chunk_done(pe, "silu_s", FC, e, c - 1, f + 1)
                    for i, (a, b) in enumerate(((0, 0), (1, 0), (0, 1))):
                        last = mm(up[f][:, 0:n], w1p[par][:, a, f * P:(f + 1) * P], xTp[sp_][:, b, 0:n], i == 0, i == 2)
                    last.then_inc(S["up_mm"], 1)

            def out_of_hidden(e, par, c, sp_):
                n = CHUNKS[c]
                chunk_done(pe, "h_lo", 2, e, c)
                chunk_done(pe, "yt_s", 1, e, c - 1)
                for f in range(FC):
                    for i, (a, b) in enumerate(((0, 0), (1, 0), (0, 1))):
                        last = mm(down[:, 0:n], w2p[par][:, a, f, :], hidp[sp_][:, b, f, 0:n],
                                  f == 0 and i == 0, f == FC - 1 and i == 2)
                last.then_inc(S["down_mm"], 1)

            def results_across(e, c, sp_):
                chunk_done(pe, "yt_s", 1, e, c)
                chunk_done(pe, "ys_s", 1, e, c - 1)
                for t, col, n in tiles_of(c):
                    last = nc.tensor.transpose(yt[0:n, (col // P) * DIM:(col // P + 1) * DIM], yT[sp_][:, col:col + n], ident)
                last.then_inc(S["yt_mm"], 1)

            def body2(e, par):
                first = isinstance(e, int) and e == 0
                for c in range(NCH):
                    s = (e_par(par) + c) % 2
                    hidden(e, par, c, s)
                    if c >= 2:
                        results_across(e, c - 2, s)
                    elif not first:
                        results_across(e - 1, c + 1, s)
                    if c < NCH - 1:
                        rows_across(e, par, c + 1)
                    else:
                        rows_across(e + 1, 1 - par, 0)
                    if c >= 1:
                        out_of_hidden(e, par, c - 1, 1 - s)
                    elif not first:
                        out_of_hidden(e - 1, 1 - par, NCH - 1, 1 - s)

            def e_par(par):
                return par * NCH

            rows_across(0, 0, 0)
            experts(pe, body2)
            e = EXPERTS - 1
            s = (NCH * EXPERTS - 1) % 2
            results_across(e, NCH - 2, 1 - s)
            out_of_hidden(e, e % 2, NCH - 1, s)
            results_across(e, NCH - 1, s)

        @block.scalar
        def _(act):
            bb, cb = bank[2:4], bank[4]
            m1, m2 = bank[6:8]

            def exponentials(k, par, u):
                if not on(k):
                    return
                after(act, "b_mm", UNITS, k, u + 1)
                after(act, "pv_mm", UNITS, k, u - 1)
                nc.scalar.activation(probs[u % 2][:], bb[u % 2][:], ACT.Exp).then_inc(S["prob_s"], 1)

            def copy_sums(j, par, p):
                if not on(j):
                    return
                after(act, "pv_mm", UNITS, j, 4 * p + 4)
                after(act, "ct_mm", 2, j - 2)
                nc.scalar.copy(csb[par][:, 2 * p:2 * p + 2, :].rearrange("p g t -> p (g t)"), cb[:]).then_inc(S["csb_s"], 1)

            def copy_maxima(j, half):
                if not on(j):
                    return
                after(act, "mt_mm", 2, j, half + 1)
                after(act, "mscr_w", 32, j - 1, 16 * half + 16)
                nc.scalar.copy(maxT[half][:], m1[0:32, 0:64].bitcast(BF16)).then_inc(S["mt_s"], 1)

            def body(k, par, pair):
                exponentials(k, par, 0)
                copy_maxima(k, 1)
                copy_sums(k - 1, 1 - par, 1)
                exponentials(k, par, 1)
                if on(k + 3):
                    after(act, "xt_mm", 1, k + 3)
                    after(act, "v_mm", 1, k + 1)
                    nc.scalar.copy(xcT[1 - par][:], m1[:]).then_inc(S["xct_s"], 1)
                if on(k - 2):
                    after(act, "xn2t_mm", 1, k - 2)
                    after(act, "logit_mm", 1, k - 3)
                    nc.scalar.copy(xn2T[:], m2[:, 0:TOKENS]).then_inc(S["xn2t_s"], 1)
                exponentials(k, par, 2)
                exponentials(k, par, 3)
                exponentials(k, par, 4)
                copy_sums(k, par, 0)
                if on(k - 2):
                    after(act, "top_s", 1, k - 2)
                    nc.scalar.activation(ediff[:], diff[:], ACT.Exp).then_inc(S["exp_gate"], 1)
                exponentials(k, par, 5)
                copy_maxima(k + 1, 0)
                exponentials(k, par, 6)
                if on(k - 1):
                    after(act, "ctxt_mm", 1, k - 1)
                    after(act, "y_mm", 1, k - 2)
                    nc.scalar.copy(ctxT[:], m1[:, 0:TOKENS]).then_inc(S["ctxt_s"], 1)
                if on(k + 3):
                    after(act, "qk_s", 1, k + 3)
                    after(act, "scr_w", 32, k + 2)
                    nc.scalar.copy(parts[:, 0, :, :], qk[:]).then_inc(S["part1"], 1)
                exponentials(k, par, 7)
                if on(k + 3):
                    after(act, "rest_s", 1, k + 3)
                    nc.scalar.copy(parts[:, 1, :, :], rest[:]).then_inc(S["part2"], 1)

            steps(act, body)

            up, down, xt = bank[0:4], bank[4], bank[5]

            def split_rows(e, c, s):
                if isinstance(e, int) and e >= EXPERTS:
                    return
                chunk_done(act, "xt2_mm", 1, e, c)
                chunk_done(act, "up_mm", FC, e, c - 2)
                nc.scalar.copy(xTp[s][:, 0, 0:CHUNKS[c]], xt[:, 0:CHUNKS[c]]).then_inc(S["xt_hi"], 1)

            def split_weights(e, par):
                if isinstance(e, int) and e >= EXPERTS:
                    return
                act.wait_ge(S["w_in"], 32 * e + 32)
                chunk_done(act, "down_mm", 1, e - 2, NCH - 1)
                nc.scalar.copy(w1p[par][:, 0, :], w1raw[par][:]).then_inc(S["w_hi"], 1)
                nc.scalar.copy(w2p[par][:, 0, :, :], w2raw[par][:]).then_inc(S["w_hi"], 1)

            def copy_results(e, c, s):
                chunk_done(act, "down_mm", 1, e, c)
                chunk_done(act, "yt_mm", 1, e, c - 2)
                nc.scalar.copy(yT[s][:, 0:CHUNKS[c]], down[:, 0:CHUNKS[c]]).then_inc(S["yt_s"], 1)

            split_weights(0, 0)
            split_rows(0, 0, 0)

            def body2(e, par):
                first = isinstance(e, int) and e == 0
                for c in range(NCH):
                    s = (par * NCH + c) % 2
                    for f in range(FC):
                        chunk_done(act, "up_mm", FC, e, c, f + 1)
                        chunk_done(act, "h_lo", 2, e, c - 2, f // 2 + 1)
                        nc.scalar.activation(hid[s][:, f, 0:CHUNKS[c]], up[f][:, 0:CHUNKS[c]], ACT.Silu
                                             ).then_inc(S["silu_s"], 1)
                    if c < NCH - 1:
                        split_rows(e, c + 1, 1 - s)
                    else:
                        split_rows(e + 1, 0, 1 - s)
                    if c >= 1:
                        copy_results(e, c - 1, 1 - s)
                    elif not first:
                        copy_results(e - 1, NCH - 1, 1 - s)
                    if c == 0:
                        split_weights(e + 1, 1 - par)
            experts(act, body2)
            copy_results(EXPERTS - 1, NCH - 1, (NCH * EXPERTS - 1) % 2)

        @block.vector
        def _(dve):
            v = nc.vector
            ab, m0, m1, m2 = bank[0:2], bank[5], bank[6], bank[7]
            desc8 = cst[:, DESC8:DESC8 + 16].rearrange("p (t e) -> p t e", t=TILES)

            def spread(ap, n):
                return ap.unsqueeze(2).to_broadcast([P, TILES, n])

            def maximum(j, par, u):
                if not on(j):
                    return
                hg, i2 = divmod(u, TILES)
                after(dve, "a_mm", UNITS, j, u + 1)
                v.reduce_max(maxima[par][:, 4 * hg:4 * hg + 4, i2],
                             ab[u % 2][:].rearrange("p (h c) -> p h c", c=P), AX).then_inc(S["max_s"], 1)

            def maximum_parts(j, par, half):
                if not on(j):
                    return
                after(dve, "max_s", UNITS, j, 4 * half + 4)
                after(dve, "mt_mm", 2, j - 1, half + 1)
                src = maxima[par][:, 8 * half:8 * half + 8, :]
                v.tensor_scalar(max_parts[half][:, 0, :, :], src, -1.0, None, ALU.mult).then_inc(S["mparts"], 1)
                after(dve, "mparts", 4, j, 2 * half + 1)
                v.scalar_tensor_tensor(max_parts[half][:, 1, :, :], src, -1.0, max_parts[half][:, 0, :, :],
                                       ALU.mult, ALU.subtract).then_inc(S["mparts"], 1)

            def normalise_stats(j, src, stats, mv, var, a, b, c):
                for t in range(TILES):
                    v.bn_stats(stats[:, t, :], src[:, t, :]).then_inc(S[a], 1)
                after(dve, a, 2, j)
                apart(dve, "past_dve")
                for t in range(TILES):
                    v.bn_aggr(mv[:, t, :], stats[:, t, :]).then_inc(S[b], 1)
                after(dve, b, 2, j)
                v.tensor_scalar(var[:], mv[:, :, 1], EPS, None, ALU.add).then_inc(S[c], 1)

            def normalise_write(dst, src, mv, rstd, name):
                for t in range(TILES):
                    v.tensor_scalar(dst(t), src[:, t, :], mv[:, t, 0:1], rstd[:, t:t + 1], ALU.subtract, ALU.mult
                                    ).then_inc(S[name], 1)

            def context(k, t, m):
                if not on(k - 1):
                    return
                after(dve, "ct_mm", 2, k - 1, t + 1)
                after(dve, "norm_s", 2, k - 2, t + 1)
                sums = m[:].rearrange("p (h c) -> p h c", c=32)
                v.reciprocal(recip[t][:], sums[:, :, HD]).then_inc(S["rec_s"], 1)
                after(dve, "rec_s", 2, k - 1, t + 1)
                after(dve, "ctxt_mm", 1, k - 2)
                v.tensor_tensor(ctxn[:, t, :].rearrange("p (h c) -> p h c", c=HD), sums[:, :, 0:HD],
                                recip[t][:].unsqueeze(2).to_broadcast([P, HEADS, HD]), ALU.mult).then_inc(S["norm_s"], 1)

            def rope(k, name, mms, m, which, c0, b0):
                if not on(k + 3):
                    return
                after(dve, mms, 1, k + 3)
                for i, dst in enumerate((straight, turned)):
                    v.scalar_tensor_tensor(dst[:, which, :], m[:, i * TOKENS:(i + 1) * TOKENS], cbias[:, b0 + i:b0 + i + 1],
                                           cst[:, c0 + i * TOKENS:c0 + (i + 1) * TOKENS], ALU.add, ALU.mult
                                           ).then_inc(S[name], 1)

            ROUTER = 17

            def choose(k):
                j = k - 2
                if not on(j):
                    return
                n = [0]

                def link(ins):
                    n[0] += 1
                    ins.then_inc(S["router"], 1)
                    after(dve, "router", ROUTER, j, n[0])
                after(dve, "logit_mm", 1, j)
                lg = m2[:, 0:16].rearrange("p (t e) -> p t e", t=TILES)
                link(v.reduce_max(top[:, 0, :], lg, AX))
                link(v.tensor_tensor(eq[:], lg, spread(top[:, 0, :], EXPERTS), ALU.is_equal))
                link(v.tensor_tensor(weighed[:], eq[:], desc8, ALU.mult))
                link(v.reduce_max(best[:, 0, :], weighed[:], AX))
                link(v.tensor_tensor(chosen[:, 0, :, :], desc8, spread(best[:, 0, :], EXPERTS), ALU.is_equal))
                link(v.tensor_scalar(weighed[:], chosen[:, 0, :, :], -3e38, None, ALU.mult))
                v.tensor_tensor(logits2[:], weighed[:], lg, ALU.add).then_inc(S["router_psum"], 1)
                after(dve, "router_psum", 1, j)
                link(v.reduce_max(top[:, 1, :], logits2[:], AX))
                v.tensor_tensor(diff[:], top[:, 1, :], top[:, 0, :], ALU.subtract).then_inc(S["top_s"], 1)
                link(v.tensor_tensor(eq[:], logits2[:], spread(top[:, 1, :], EXPERTS), ALU.is_equal))
                link(v.tensor_tensor(weighed[:], eq[:], desc8, ALU.mult))
                link(v.reduce_max(best[:, 1, :], weighed[:], AX))
                link(v.tensor_tensor(chosen[:, 1, :, :], desc8, spread(best[:, 1, :], EXPERTS), ALU.is_equal))
                after(dve, "prefix_mm", 1, j - 1)
                v.tensor_tensor(both16[:], chosen[:, 0, :, :], chosen[:, 1, :, :], ALU.add).then_inc(S["both_s"], 1)

            def rank(k, par):
                j = k - 2
                if not on(j):
                    return
                n = [11]

                def link(ins):
                    n[0] += 1
                    ins.then_inc(S["router"], 1)
                    after(dve, "router", ROUTER, j, n[0])
                after(dve, "prefix_mm", 1, j)
                dve.wait_ge(S["counted"], 1)
                after(dve, "ranked", 1, j - 1)
                link(v.tensor_tensor(place[:], m0[:, 0:16].rearrange("p (t e) -> p t e", t=TILES),
                                     count[:].unsqueeze(1).to_broadcast([P, TILES, EXPERTS]), ALU.add))
                v.tensor_tensor(count[:], count[:], m0[:, 16:24], ALU.add).then_inc(S["ranked"], 1)
                link(v.tensor_tensor(over[:], place[:], cst[:, LIMIT:LIMIT + 8].unsqueeze(1).to_broadcast(
                    [P, TILES, EXPERTS]), ALU.is_ge))
                link(v.scalar_tensor_tensor(place2[:], over[:], FAR, place[:], ALU.mult, ALU.add))
                link(v.tensor_tensor(picked[:], chosen[:], place2[:].unsqueeze(1).to_broadcast(
                    [P, 2, TILES, EXPERTS]), ALU.mult))
                after(dve, "exp_gate", 1, j)
                link(v.tensor_scalar(gate[:, 0, :], ediff[:], 1.0, None, ALU.add))
                with nc.allow_low_precision(reason="places are whole numbers below 2**24"):
                    v.reduce_sum(index[par][:], picked[:].rearrange("p s t e -> p (s t) e"), AX
                                 ).then_inc(S["gate_s"], 1)
                link(v.reciprocal(gate[:, 1, :], gate[:, 0, :]))
                v.tensor_copy(rows[par][:, 0, :, DIM], gate[:, 1, :]).then_inc(S["gate_s"], 1)
                v.tensor_tensor(rows[par][:, 1, :, DIM], gate[:, 1, :], ediff[:], ALU.mult).then_inc(S["gate_s"], 1)

            v.memset(v_sb[0][:], 0.0).then_inc(S["v_ones"], 1)
            v.memset(v_sb[1][:], 0.0).then_inc(S["v_ones"], 1)
            dve.wait_ge(S["v_ones"], 2)
            v.memset(v_sb[0][:, :, :, HD:2 * HD], 1.0).then_inc(S["v_ones"], 1)
            v.memset(v_sb[1][:, :, :, HD:2 * HD], 1.0).then_inc(S["v_ones"], 1)
            dve.wait_ge(S["v_ones"], 4)

            def body(k, par, pair):
                maximum_parts(k, par, 1)
                maximum(k + 1, 1 - par, 0)
                if on(k + 1):
                    after(dve, "v_mm", 1, k + 1)
                    after(dve, "pv_mm", UNITS, k - 1)
                    v.tensor_tensor(v_sb[1 - par][:, :, :, 0:HD],
                                    m0[:, 0:3 * P].rearrange("p (a h c) -> p a h c", a=3, c=HD),
                                    rbias[:, 0, :].rearrange("p (h c) -> p h c", c=HD).unsqueeze(1).to_broadcast(
                                        [P, 3, HEADS, HD]), ALU.add).then_inc(S["v_s"], 1)
                maximum(k + 1, 1 - par, 1)
                maximum(k + 1, 1 - par, 2)
                context(k, 0, m0)
                choose(k)
                maximum(k + 1, 1 - par, 3)
                context(k, 1, m1)
                rope(k, "roped_q", "q_mm", m0, 0, COSQ, 0)
                maximum_parts(k + 1, 1 - par, 0)
                maximum(k + 1, 1 - par, 4)
                rope(k, "roped_k", "k_mm", m2, 1, COSK, 2)
                if on(k + 3):
                    after(dve, "roped_q", 2, k + 3)
                    after(dve, "roped_k", 2, k + 3)
                    after(dve, "part1", 1, k + 2)
                    after(dve, "rest_s", 1, k + 2)
                    v.tensor_tensor(qk[:], straight[:], turned[:], ALU.add).then_inc(S["qk_s"], 1)
                maximum(k + 1, 1 - par, 5)
                rank(k, par)
                maximum(k + 1, 1 - par, 6)
                if on(k + 4):
                    after(dve, "x_in", 16, k + 4)
                    after(dve, "rstd1_s", 1, k + 3)
                    normalise_stats(k + 4, xin[par], stats1, mv1, var1, "stats1_s", "mv1_s", "var1_s")
                if on(k - 1):
                    after(dve, "y_mm", 1, k - 1)
                    after(dve, "xrb_s", 1, k - 1)
                    after(dve, "base_s", 1, k - 3)
                    v.tensor_tensor(x1[1 - par][:].rearrange("p t c -> p (t c)"),
                                    xres[1 - par][:].rearrange("p t c -> p (t c)"), m2[:, 0:TOKENS], ALU.add
                                    ).then_inc(S["x1_s"], 1)
                    after(dve, "x1_s", 1, k - 1)
                    after(dve, "rstd2_s", 1, k - 2)
                    normalise_stats(k - 1, x1[1 - par], stats2, mv2, var2, "stats2_s", "mv2_s", "var2_s")
                if on(k + 4):
                    after(dve, "rstd1_s", 1, k + 4)
                    after(dve, "xt_mm", 1, k + 2)
                    normalise_write(lambda t: xn1[par][:, t, :], xin[par], mv1, rstd1, "xn1_s")
                maximum(k + 1, 1 - par, 7)
                if on(k - 1):
                    after(dve, "rstd2_s", 1, k - 1)
                    after_same(dve, "scattered", 64, par, pair, -3)
                    after_same(dve, "base_out", 16, par, pair, -3)
                    normalise_write(lambda t: rows[1 - par][:, 0, t, 0:DIM], x1[1 - par], mv2, rstd2, "xn2_s")
            steps(dve, body)

            xt, yt = bank[5], bank[6]

            def rest_of_rows(e, c, s):
                if isinstance(e, int) and e >= EXPERTS:
                    return
                chunk_done(dve, "xt_hi", 1, e, c)
                v.tensor_tensor(xTp[s][:, 1, 0:CHUNKS[c]], xt[:, 0:CHUNKS[c]], xTp[s][:, 0, 0:CHUNKS[c]].bitcast(F32),
                                ALU.subtract).then_inc(S["xt_lo"], 1)

            def rest_of_weights(e, par):
                if isinstance(e, int) and e >= EXPERTS:
                    return
                dve.wait_ge(S["w_hi"], 2 * e + 2)
                v.tensor_tensor(w1p[par][:, 1, :], w1raw[par][:], w1p[par][:, 0, :].bitcast(F32), ALU.subtract
                                ).then_inc(S["w_lo"], 1)
                v.tensor_tensor(w2p[par][:, 1, :, :], w2raw[par][:], w2p[par][:, 0, :, :].bitcast(F32), ALU.subtract
                                ).then_inc(S["w_lo"], 1)

            def weigh_results(e, par, c, s):
                chunk_done(dve, "yt_mm", 1, e, c)
                back, since = (c - 2) % NCH, e if c >= 2 else e - 1
                if not isinstance(e, int) or since >= 0:
                    each = 16 * len(tiles_of(back))
                    dve.wait_ge(S[f"added{back}"], since * each + each)
                full = [t for t in tiles_of(c) if t[2] == P]
                part = [t for t in tiles_of(c) if t[2] < P]
                t0, m = full[0][0], len(full)
                ins = v.tensor_tensor(ys[s][:, 0:m, :], yt[:, 0:m * DIM].rearrange("p (t c) -> p t c", c=DIM),
                                      xs[par][:, t0:t0 + m, DIM:DIM + 1].to_broadcast([P, m, DIM]), ALU.mult)
                for t, col, n in part:
                    i = col // P
                    ins = v.tensor_tensor(ys[s][0:n, i, :], yt[0:n, i * DIM:(i + 1) * DIM],
                                          xs[par][0:n, t, DIM:DIM + 1].to_broadcast([n, DIM]), ALU.mult)
                ins.then_inc(S["ys_s"], 1)

            rest_of_weights(0, 0)
            rest_of_rows(0, 0, 0)

            def body2(e, par):
                first = isinstance(e, int) and e == 0
                for c in range(NCH):
                    s = (par * NCH + c) % 2
                    if c >= 2:
                        weigh_results(e, par, c - 2, s)
                    elif not first:
                        weigh_results(e - 1, 1 - par, c + 1, s)
                    for g in range(2):
                        chunk_done(dve, "silu_s", FC, e, c, 2 * g + 2)
                        chunk_done(dve, "down_mm", 1, e, c - 2)
                        src = hid[s][:, 2 * g:2 * g + 2, 0:CHUNKS[c]]
                        v.tensor_copy(hidp[s][:, 0, 2 * g:2 * g + 2, 0:CHUNKS[c]], src).then_inc(S["h_hi"], 1)
                        chunk_done(dve, "h_hi", 2, e, c, g + 1)
                        v.tensor_tensor(hidp[s][:, 1, 2 * g:2 * g + 2, 0:CHUNKS[c]], src,
                                        hidp[s][:, 0, 2 * g:2 * g + 2, 0:CHUNKS[c]].bitcast(F32), ALU.subtract
                                        ).then_inc(S["h_lo"], 1)
                    if c < NCH - 1:
                        rest_of_rows(e, c + 1, 1 - s)
                    else:
                        rest_of_rows(e + 1, 0, 1 - s)
                    if c == 0:
                        rest_of_weights(e + 1, 1 - par)
            experts(dve, body2)
            e = EXPERTS - 1
            s = (NCH * EXPERTS - 1) % 2
            weigh_results(e, e % 2, NCH - 2, 1 - s)
            weigh_results(e, e % 2, NCH - 1, s)

        @block.gpsimd
        def _(pool):
            g = nc.gpsimd
            g.memset(empty[:], 0.0).then_inc(S["init_made"], 1)
            g.memset(half_neg[:], -0.5).then_inc(S["half_set"], 1)
            pool.wait_ge(S["init_made"], 1)
            pool.dma_start(out[ALL:ALL + QUEUE, :].rearrange("(p r) c -> p r c", p=INIT_P),
                           empty[:, :, 0:DIM]).then_inc(S["dump_out"], 16)
            g.iota(empty[:, :, DIM + 1].bitcast(I32), pattern=[[1, INIT_R]], base=ALL, channel_multiplier=INIT_R
                   ).then_inc(S["init_made"], 1)
            pool.wait_ge(S["init_made"], 2)
            for e in range(EXPERTS):
                pool.dma_start(queues[e * QUEUE:(e + 1) * QUEUE, :].rearrange("(p r) c -> p r c", p=INIT_P),
                               empty[:]).then_inc(S["init_out"], 16)
            pool.wait_ge(S["consts_in"], CONST_LOADS)
            g.tensor_copy(count[:], cst[:, START:START + 8]).then_inc(S["counted"], 1)
            g.tensor_copy(tok[:], cst[:, TOK:TOK + 2]).then_inc(S["half_set"], 1)
            pool.wait_ge(S["half_set"], 2)

            def body(k, par, pair):
                if isinstance(k, int) and k == 1:
                    pool.wait_ge(S["init_out"], 16 * EXPERTS)
                if on(k - 2):
                    j = k - 2
                    after(pool, "xn2_s", 2, j)
                    apart(pool, "past_pool")
                    g.tensor_copy(rows[par][:, 1, :, 0:DIM], rows[par][:, 0, :, 0:DIM]).then_inc(S["rowcopy_s"], 1)
                    g.tensor_tensor(base[par][:], x1[par][:], rows[par][:, 0, :, 0:DIM], ALU.add).then_inc(S["base_s"], 1)
                    after(pool, "tok_s", 2, j - 1)
                    apart(pool, "past_pool")
                    g.tensor_copy(rows[par][:, :, :, DIM + 1].bitcast(I32),
                                  tok[:].unsqueeze(1).to_broadcast([P, 2, TILES])).then_inc(S["tok_s"], 1)
                    after(pool, "tok_s", 2, j, 1)
                    apart(pool, "past_pool")
                    g.tensor_scalar(tok[:], tok[:], float(TOKENS), None, ALU.add).then_inc(S["tok_s"], 1)
                if on(k - 1):
                    after(pool, "xr_in", 16, k - 1)
                    g.tensor_tensor(xres[1 - par][:], xres[1 - par][:],
                                    rbias[:, 1, :].unsqueeze(1).to_broadcast([P, TILES, DIM]), ALU.add
                                    ).then_inc(S["xrb_s"], 1)
                if on(k + 4):
                    after(pool, "var1_s", 1, k + 4)
                    after(pool, "xn1_s", 2, k + 3)
                    g.tensor_tensor(rstd1[:], var1[:], half_neg[:], ALU.pow).then_inc(S["rstd1_s"], 1)
                if on(k + 3):
                    after(pool, "part1", 1, k + 3)
                    after(pool, "part2", 1, k + 2)
                    g.tensor_tensor(rest[:], qk[:], parts[:, 0, :, :], ALU.subtract).then_inc(S["rest_s"], 1)
                if on(k - 1):
                    after(pool, "var2_s", 1, k - 1)
                    after(pool, "xn2_s", 2, k - 2)
                    g.tensor_tensor(rstd2[:], var2[:], half_neg[:], ALU.pow).then_inc(S["rstd2_s"], 1)
                if on(k + 3):
                    after(pool, "part2", 1, k + 3)
                    g.tensor_tensor(parts[:, 2, :, :], rest[:], parts[:, 1, :, :], ALU.subtract).then_inc(S["part3"], 1)
                if on(k - 2):
                    j = k - 2
                    after(pool, "gate_s", 3, j)
                    after(pool, "rowcopy_s", 1, j)
                    after(pool, "tok_s", 2, j)
                    apart(pool, "past_pool")
                    for n in range(2 * TILES):
                        g.indirect_dma_start(queues, bass.IndirectOffsetOnAxis(ap=index[par][:, n:n + 1], axis=0),
                                             rows[par][:, n // TILES, n % TILES, :], None,
                                             bounds_check=EXPERTS * QUEUE - 1, oob_is_err=False).then_inc(S[f"scattered{par}"], 16)
            steps(pool, body)

            for n in range(2):
                pool.wait_ge(S[f"base_out{n}"], 16 * BATCHES // 2)
            pool.wait_ge(S["dump_out"], 16)

            def body2(e, par):
                for c in range(NCH):
                    s = (par * NCH + c) % 2
                    chunk_done(pool, "ys_s", 1, e, c)
                    if c == 0 and (not isinstance(e, int) or e > 0):
                        added_all(pool, e)
                    apart(pool, "past_pool")
                    for t, col, n in tiles_of(c):
                        g.indirect_dma_start(out, bass.IndirectOffsetOnAxis(
                            ap=xs[par][0:n, t, DIM + 1:DIM + 2].bitcast(I32), axis=0),
                            ys[s][0:n, col // P, :], None, compute_op=ALU.add).then_inc(S[f"added{c}"], 16)
            experts(pool, body2)
            added_all(pool, EXPERTS)


def shape_constants():
    f = np.float32
    c = np.zeros((P, CONSTS), f)
    c[:, IDENT:IDENT + P] = np.eye(P, dtype=f)
    half = HD // 2
    freqs = (f(1.0) / f(10000.0) ** (np.arange(half, dtype=f) / f(half))).astype(f)
    ang = np.arange(TOKENS, dtype=f)[None, :] * freqs[(np.arange(P) // HEADS) % half][:, None]
    cos, sin = np.cos(ang).astype(f), np.sin(ang).astype(f)
    sin = np.where((np.arange(P) // HEADS < half)[:, None], -sin, sin)
    scale = f(HD ** -0.5)
    c[:, COSQ:COSQ + TOKENS], c[:, SINQ:SINQ + TOKENS] = cos * scale, sin * scale
    c[:, COSK:COSK + TOKENS], c[:, SINK:SINK + TOKENS] = cos, sin
    e = np.arange(EXPERTS)
    c[:, DESC8:DESC8 + 16] = np.tile(EXPERTS - e, 2)
    c[:, LIMIT:LIMIT + 8] = e * QUEUE + CAPACITY
    c[:, START:START + 8] = e * QUEUE
    c[:, TOK:TOK + 2] = np.arange(P)[:, None] + np.arange(TILES) * P
    c16 = np.zeros((P, 3 * P), f)
    c16[:, 0:P] = np.eye(P)
    c16[:, P:2 * P] = np.triu(np.ones((P, P)), 1)
    c16[:, 2 * P:] = 1
    t = np.arange(TOKENS)
    q = np.zeros((CONST_ROWS, TOKENS), f)
    q[0] = t < BLOCK
    q[64 - FLAG_ROW:] = (t % BLOCK)[None, :] == np.arange(BLOCK)[:, None]
    k = np.zeros((CONST_ROWS, 2, TOKENS), f)
    k[0] = np.where(t // BLOCK == 1, MASKED, 0)
    k[1:3] = 1
    j, r = np.arange(BLOCK)[:, None], (t % BLOCK)[None, :]
    for odd in range(2):
        under = (t // BLOCK % 2 == odd)[None, :]
        k[64 - FLAG_ROW:, odd] = np.where(np.where(under, r <= j, r >= j), 0, MASKED)
    b = mybir.dt.np(BF16)
    return c, c16.astype(b), q.astype(b), k.astype(b)


def kernel(x, ctx_1024, L0_xattn_q_w, L0_xattn_q_b, L0_xattn_k_w, L0_xattn_k_b, L0_xattn_v_w, L0_xattn_v_b,
           L0_xattn_o_w, L0_xattn_o_b, L0_ffn_router_w, L0_ffn_w1, L0_ffn_w2):
    import concourse.bacc as bacc
    from concourse.bass_utils import run_bass_kernel_spmd

    def by_dim(w, turn):
        a = np.asarray(w).reshape((HEADS, HD) + np.asarray(w).shape[1:])
        if turn:
            a = np.concatenate([a[:, HD // 2:], a[:, :HD // 2]], axis=1)
        a = np.swapaxes(a, 0, 1)
        return a.reshape((DIM,) + a.shape[2:])

    qw, kw = np.asarray(L0_xattn_q_w), np.asarray(L0_xattn_k_w)
    weights = np.concatenate([by_dim(qw, False).T, by_dim(qw, True).T, by_dim(kw, False).T, by_dim(kw, True).T,
                              np.asarray(L0_xattn_v_w).T, np.asarray(L0_xattn_o_w).T,
                              np.asarray(L0_ffn_router_w).T], axis=1)
    qb, kb = np.asarray(L0_xattn_q_b), np.asarray(L0_xattn_k_b)
    col_bias = np.stack([by_dim(qb, False), by_dim(qb, True), by_dim(kb, False), by_dim(kb, True)], axis=1)
    row_bias = np.stack([np.asarray(L0_xattn_v_b), np.asarray(L0_xattn_o_b)])
    c, c16, q_rows, k_rows = shape_constants()
    arrays = {"x": x, "ctx": ctx_1024, "weights": weights, "col_bias": col_bias, "row_bias": row_bias,
              "consts": c, "consts16": c16, "q_rows": q_rows, "k_rows": k_rows, "w1": L0_ffn_w1, "w2": L0_ffn_w2}
    arrays = {f"in_{n}": np.ascontiguousarray(a) for n, a in arrays.items()}
    nc = bacc.Bacc("TRN2", target_bir_lowering=False, num_devices=1)
    ins = [nc.dram_tensor(n, a.shape, mybir.dt.from_np(a.dtype), kind="ExternalInput").ap() for n, a in arrays.items()]
    out = nc.dram_tensor("out", [ALL + QUEUE, DIM], F32, kind="ExternalOutput").ap()
    build(nc, *ins, out)
    r = run_bass_kernel_spmd(nc, [arrays], core_ids=[0])
    return r.results[0]["out"][:ALL].reshape(BATCHES, TOKENS, DIM)
```

```python
from contextlib import ExitStack

import numpy as np

import concourse.bass as bass
from concourse import mybir

F32 = mybir.dt.float32
F32R = mybir.dt.float32r
BF16 = mybir.dt.bfloat16
I32 = mybir.dt.int32
U32 = mybir.dt.uint32
ALU = mybir.AluOpType
ACT = mybir.ActivationFunctionType
AX = mybir.AxisListType.X

P = 128
BATCHES = 16
TOKENS = 256
CONTEXT = 1601
DIM = 128
HEADS = 16
HD = DIM // HEADS
BLOCK = 64
TILES = TOKENS // P
GROUPS = HEADS // 4
UNITS = GROUPS * TILES
EXPERTS = 8
HIDDEN = 512
ALL = BATCHES * TOKENS
CAPACITY = int(1.25 * ALL * 2 / EXPERTS) + 1
QUEUE = 1344
INIT_P = 64
INIT_R = QUEUE // INIT_P
USED = 1284
ROW = DIM + 2
EPS = 1e-5
MASKED = -1e30
FAR = float(1 << 20)
PARTS = 3
PAIRS = 6
FLAG_ROW = PAIRS * HD
MAX_ROWS = FLAG_ROW + 1
CONST_ROWS = P - FLAG_ROW
MASK_ROW = 64
KEY_TILE = [0, 0, 1, 2]

CHUNKS = [512, 512, USED - 1024]
FC = HIDDEN // P

IDENT, COSQ, SINQ, COSK, SINK = 0, P, P + TOKENS, P + 2 * TOKENS, P + 3 * TOKENS
EXPERT = P + 4 * TOKENS
LIMIT = EXPERT + 8
START = LIMIT + 8
TOK = START + 8
CONSTS = TOK + 2
WQ, WQR, WK, WKR, WV, WO, WR = (n * DIM for n in range(7))
WEIGHTS = WR + EXPERTS


def build(nc, x, ctx_in, weights, col_bias, row_bias, consts, consts16, q_rows, k_rows, w1, w2, out):
    scr_q = nc.dram_tensor("q_scratch", [2, MAX_ROWS + 2, HEADS * TOKENS], BF16).ap()
    scr_k = nc.dram_tensor("k_scratch", [2, FLAG_ROW, HEADS * TOKENS], BF16).ap()
    scr_m = nc.dram_tensor("maxima_scratch", [2, 2, 2, 16 * P], BF16).ap()
    queues = nc.dram_tensor("queues", [EXPERTS * QUEUE, ROW], F32).ap()

    es = ExitStack()
    with es:
        def sb(name, shape, dt=F32):
            return es.enter_context(nc.sbuf_tensor(name, shape, dt))

        def two(name, shape, dt=F32):
            return [sb(f"{name}{n}", shape, dt) for n in range(2)]

        def sem(name):
            return es.enter_context(nc.semaphore(name))

        bank = [es.enter_context(nc.psum_tensor(f"bank{n}", [P, 512], F32)) for n in range(8)]

        cst = sb("cst", [P, CONSTS])
        cst16 = sb("cst16", [P, 3 * P], BF16)
        wts = sb("wts", [P, WEIGHTS])
        cbias = sb("cbias", [P, 5])
        rbias = sb("rbias", [P, DIM])
        ident = cst[:, IDENT:IDENT + P]
        ident16, earlier16, ones16 = (cst16[:, n * P:(n + 1) * P] for n in range(3))
        count = sb("count", [P, EXPERTS])
        tok = sb("tok", [P, TILES])
        half_neg = sb("half_neg", [P, TILES])

        xin = two("xin", [P, TILES, DIM])
        cin = two("cin", [P, TILES, DIM])
        xn1 = two("xn1", [P, TILES, DIM])
        stats1 = sb("stats1", [P, TILES, 6])
        mv1 = sb("mv1", [P, TILES, 2])
        var1 = sb("var1", [P, TILES])
        rstd1 = sb("rstd1", [P, TILES])
        xcT = two("xcT", [P, 2 * TOKENS])
        straight = sb("straight", [P, 2, TOKENS])
        turned = sb("turned", [P, 2, TOKENS])
        qk = sb("qk", [P, 2, TOKENS])
        rest = sb("rest", [P, 2, TOKENS])
        parts = sb("parts", [P, PARTS, 2, TOKENS], BF16)
        v_sb = two("v_sb", [P, 3, HEADS, 32])
        maxima = two("maxima", [P, HEADS, TILES])
        max_parts = two("max_parts", [P, 2, 8, TILES], BF16)
        maxT = two("maxT", [2 * 8 * TILES, P], BF16)
        probs = two("probs", [P, 512])
        csb = two("csb", [P, GROUPS, TOKENS])
        recip = two("recip", [P, HEADS])
        ctxn = sb("ctxn", [P, TILES, DIM])
        ctxT = sb("ctxT", [P, TOKENS])
        xres = two("xres", [P, TILES, DIM])
        x1 = two("x1", [P, TILES, DIM])
        stats2 = sb("stats2", [P, TILES, 6])
        mv2 = sb("mv2", [P, TILES, 2])
        var2 = sb("var2", [P, TILES])
        rstd2 = sb("rstd2", [P, TILES])
        rows = two("rows", [P, 2, TILES, ROW])
        base = two("base", [P, TILES, DIM])
        xn2T = sb("xn2T", [P, TOKENS])
        top = sb("top", [P, TILES, 8])
        diff = sb("diff", [P, TILES])
        ediff = sb("ediff", [P, TILES])
        gate = sb("gate", [P, 2, TILES])
        top_index = sb("top_index", [P, TILES, 8], U32)
        chosen = sb("chosen", [P, 2, TILES, EXPERTS])
        both16 = sb("both16", [P, TILES, EXPERTS], BF16)
        place = sb("place", [P, TILES, EXPERTS])
        over = sb("over", [P, TILES, EXPERTS])
        place2 = sb("place2", [P, TILES, EXPERTS])
        picked = sb("picked", [P, 2, TILES, EXPERTS])
        index = two("index", [P, 2 * TILES], I32)
        mask_rows = sb("mask_rows", [P, 3, TOKENS], BF16)
        empty = sb("empty", [INIT_P, INIT_R, ROW])

        xs = two("xs", [P, 11, ROW])
        row_gate = two("row_gate", [P, 11])
        row_token = two("row_token", [P, 11], I32)
        w1raw = two("w1raw", [P, HIDDEN])
        w2raw = two("w2raw", [P, FC, DIM])
        w1p = two("w1p", [P, 2, HIDDEN], F32R)
        w2p = two("w2p", [P, 2, FC, DIM], F32R)
        xTp = two("xTp", [P, 2, 512], F32R)
        yT = two("yT", [P, 512])
        ys = two("ys", [P, 4, DIM])
        with ExitStack() as packs:
            def pack_buffers(name, shape):
                return [packs.enter_context(nc.sbuf_tensor(f"{name}{n}", shape, BF16)) for n in range(2)]

            q_pack = pack_buffers("q_pack", [P, HEADS, TOKENS])
            k_pack = pack_buffers("k_pack", [P, 2, HEADS, TOKENS])
        hid = two("hid", [P, FC, 512])
        hidp = two("hidp", [P, 2, FC, 512], F32R)

        S = {}
        for name in """consts_in masks_in pack_rows_in masks_made vbias_mm obias_s x_in c_in init_made init_out dump_out v_ones counted half_set
            stats1_s mv1_s var1_s rstd1_s xn1_s xt_mm xct_s q_mm k_mm roped_q roped_k qk_s part1 rest_s part2 part3
            scr_w packed0 packed1 a_mm max_s mparts mt_mm mt_s mscr_w m_packed0 m_packed1 v_mm v_s b_mm prob_s pv_mm csb_s
            ct_mm rec_s norm_s ctxt_mm ctxt_s y_mm xr_in xrb_s x1_s stats2_s mv2_s var2_s rstd2_s xn2_s
            rowcopy_s base_s tok_s base_out0 base_out1 xn2t_mm xn2t_s logit_mm top_s exp_gate gate_s both_s prefix_mm ranked
            router indexed past_dve past_pool past_sp scattered0 scattered1
            xs_in tags_s w_in w_hi w_lo xt2_mm xt_hi xt_lo up_mm silu_s h_hi h_lo down_mm yt_s yt_mm ys_s added0 added1 added2""".split():
            S[name] = sem(name)

        block = es.enter_context(nc.Block())

        def after(eng, name, per, batch, n=None):
            n = per if n is None else n
            if isinstance(batch, int):
                if batch >= BATCHES:
                    batch, n = BATCHES - 1, per
                if batch * per + n <= 0:
                    return
            eng.wait_ge(S[name], batch * per + n)

        def after_same(eng, name, per, par, pair, ahead):
            n = pair + (par + ahead) // 2
            if not isinstance(n, int) or n >= 0:
                eng.wait_ge(S[f"{name}{(par + ahead) % 2}"], n * per + per)

        CONST_LOADS = 5 * 16
        PACK_ROWS = 8 * 16
        ROUTER = 9

        def apart(eng, name):
            eng.sem_inc(S[name], 1)

        def on(batch):
            return not isinstance(batch, int) or 0 <= batch < BATCHES

        FIRST, LOOP, END, LAST = -4, 2, 10, 18

        def steps(eng, body):
            for k in range(FIRST, LOOP):
                body(k, k % 2, k // 2)
            with eng.Fori(0, (END - LOOP) // 2) as n:
                body(n * 2 + LOOP, 0, n + LOOP // 2)
                body(n * 2 + (LOOP + 1), 1, n + LOOP // 2)
            for k in range(END, LAST):
                body(k, k % 2, k // 2)

        EX_LOOP, EX_END = 1, 7

        def experts(eng, body):
            body(0, 0)
            with eng.Fori(0, (EX_END - EX_LOOP) // 2) as n:
                body(n * 2 + EX_LOOP, 1)
                body(n * 2 + (EX_LOOP + 1), 0)
            body(7, 1)

        NCH = len(CHUNKS)

        def chunk_done(eng, name, per, e, c, n=None):
            n = per if n is None else n
            v = (e * NCH + c) * per + n
            if isinstance(e, int) and v <= 0:
                return
            eng.wait_ge(S[name], v)

        def added_all(eng, e):
            for c in range(NCH):
                eng.wait_ge(S[f"added{c}"], e * (16 * len(tiles_of(c))))

        def tiles_of(c):
            return [(4 * c + t, t * P, min(P, CHUNKS[c] - t * P)) for t in range(-(-CHUNKS[c] // P))]

        @block.sync
        def _(sp):
            def load_x(j, par):
                if not on(j):
                    return
                after(sp, "xn1_s", 2, j - 2)
                apart(sp, "past_sp")
                after(sp, "stats1_s", 2, j - 1)
                apart(sp, "past_sp")
                sp.dma_start(xin[par][:], x[j, :, :].rearrange("(t p) c -> p t c", p=P)).then_inc(S["x_in"], 16)

            def load_context(j, par):
                if not on(j):
                    return
                after(sp, "xt_mm", 1, j - 1)
                apart(sp, "past_sp")
                sp.dma_start(cin[par][:], ctx_in[j, 0:TOKENS, :].rearrange("(t p) c -> p t c", p=P)).then_inc(S["c_in"], 16)

            load_x(0, 0)
            load_context(0, 0)
            sp.dma_start(cst[:], consts).then_inc(S["consts_in"], 16)
            sp.dma_start(wts[:], weights).then_inc(S["consts_in"], 16)
            sp.dma_start(cbias[:], col_bias).then_inc(S["consts_in"], 16)
            sp.dma_start(rbias[:], row_bias.unsqueeze(0).to_broadcast([P, DIM])).then_inc(S["consts_in"], 16)
            sp.dma_start(cst16[:], consts16).then_inc(S["consts_in"], 16)
            sp.dma_start(mask_rows[MASK_ROW:P, 0, :], q_rows[MASK_ROW - FLAG_ROW:, :]).then_inc(S["masks_in"], 16)
            sp.dma_start(mask_rows[MASK_ROW:P, 1:3, :], k_rows[MASK_ROW - FLAG_ROW:, :, :]).then_inc(S["masks_in"], 16)
            load_x(1, 1)
            for n in range(2):
                sp.dma_start(scr_q[n, FLAG_ROW:MAX_ROWS + 2, :].rearrange("r (h t) -> r h t", h=HEADS),
                             q_rows[0:3, :].unsqueeze(1).to_broadcast([3, HEADS, TOKENS])).then_inc(S["pack_rows_in"], 16)
                sp.dma_start(q_pack[n][MAX_ROWS + 2:MASK_ROW, :, :],
                             q_rows[3:MASK_ROW - FLAG_ROW, :].unsqueeze(1).to_broadcast(
                                 [MASK_ROW - MAX_ROWS - 2, HEADS, TOKENS])).then_inc(S["pack_rows_in"], 16)
                for v in range(2):
                    sp.dma_start(k_pack[n][FLAG_ROW:MASK_ROW, v, :, :],
                                 k_rows[0:MASK_ROW - FLAG_ROW, v, :].unsqueeze(1).to_broadcast(
                                     [MASK_ROW - FLAG_ROW, HEADS, TOKENS])).then_inc(S["pack_rows_in"], 16)

            def empty_queues(first, last):
                for e in range(first, last):
                    sp.dma_start(queues[e * QUEUE:(e + 1) * QUEUE, :].rearrange("(p r) c -> p r c", p=INIT_P),
                                 empty[:]).then_inc(S["init_out"], 16)

            load_context(1, 1)
            sp.wait_ge(S["init_made"], 2)
            sp.dma_start(out[ALL:ALL + QUEUE, :].rearrange("(p r) c -> p r c", p=INIT_P),
                         empty[:, :, 0:DIM]).then_inc(S["dump_out"], 16)
            empty_queues(0, 2)
            REST_OF_QUEUES = [(2, 4), (4, 6), (6, 7), (7, 8)]

            def parts_out(j, par, s):
                if not on(j):
                    return
                to = (scr_q, scr_k)[s][par, 0:FLAG_ROW, :].rearrange("(n d) (h t) -> (d h) n t", n=PAIRS, h=HEADS)
                if s == 0:
                    for half in range(2):
                        after(sp, f"packed{half}", 32, j - 2)
                        apart(sp, "past_sp")
                    after(sp, "part3", 1, j)
                    apart(sp, "past_sp")
                    for part, at, times in ((0, 0, 3), (1, 3, 2), (2, 5, 1)):
                        sp.dma_start(to[:, at:at + times, :],
                                     parts[:, part, 0, :].unsqueeze(1).to_broadcast([P, times, TOKENS])
                                     ).then_inc(S["scr_w"], 16)
                else:
                    for at, run in ((0, 3), (3, 2), (5, 1)):
                        sp.dma_start(to[:, at:at + run, :], parts[:, 0:run, 1, :]).then_inc(S["scr_w"], 16)

            def pack(j, par, half):
                if not on(j):
                    return
                after(sp, "scr_w", 96, j)
                apart(sp, "past_sp")
                after(sp, "b_mm", UNITS, j - 2, 4 * half + 4)
                apart(sp, "past_sp")
                hs = slice(8 * half, 8 * half + 8)
                cs = slice(8 * half * TOKENS, (8 * half + 8) * TOKENS)
                sp.dma_start(q_pack[par][0:MAX_ROWS + 2, hs, :].rearrange("p h t -> p (h t)"), scr_q[par, :, cs]
                             ).then_inc(S[f"packed{half}"], 16)
                sp.dma_start(k_pack[par][0:FLAG_ROW, :, hs, :].rearrange("p v h t -> p v (h t)"),
                             scr_k[par, :, cs].unsqueeze(1).to_broadcast([FLAG_ROW, 2, 8 * TOKENS])
                             ).then_inc(S[f"packed{half}"], 16)

            def maxima_out(j, par, half):
                if not on(j):
                    return
                after(sp, "mt_s", 2, j, half + 1)
                apart(sp, "past_sp")
                after(sp, f"m_packed{half}", 16, j - 2)
                sp.dma_start(scr_m[par, half].rearrange("s (r q) -> (s r) q", q=P), maxT[half][:]).then_inc(S["mscr_w"], 16)

            def maxima_in(j, par, half):
                if not on(j):
                    return
                after(sp, "mscr_w", 32, j, 16 * half + 16)
                sp.dma_start(q_pack[par][MAX_ROWS:MAX_ROWS + 2, 8 * half:8 * half + 8, :].rearrange("p h t -> p (h t)"),
                             scr_m[par, half]).then_inc(S[f"m_packed{half}"], 16)

            def body(k, par, pair):
                other = 1 - par
                if isinstance(k, int) and k == -2:
                    sp.wait_ge(S["pack_rows_in"], PACK_ROWS)
                pack(k + 1, other, 1)
                maxima_out(k, par, 1)
                parts_out(k + 2, par, 0)
                maxima_in(k, par, 1)
                parts_out(k + 2, par, 1)
                if not (isinstance(k, int) and k == FIRST):
                    if not (isinstance(k, int) and k == FIRST + 1):
                        load_context(k + 4, par)
                    load_x(k + 5, other)
                maxima_out(k + 1, other, 0)
                pack(k + 2, par, 0)
                if on(k - 2):
                    after(sp, "base_s", 1, k - 2)
                    sp.dma_start(out[bass.ds((k - 2) * TOKENS, TOKENS), :].rearrange("(t p) c -> p t c", p=P),
                                 base[par][:]).then_inc(S[f"base_out{par}"], 16)
                maxima_in(k + 1, other, 0)
                if on(k):
                    after(sp, "x1_s", 1, k - 2)
                    apart(sp, "past_sp")
                    after(sp, "xrb_s", 1, k - 1)
                    apart(sp, "past_sp")
                    sp.dma_start(xres[par][:], x[k, :, :].rearrange("(t p) c -> p t c", p=P)).then_inc(S["xr_in"], 16)
                if isinstance(k, int) and -2 <= k < LOOP:
                    empty_queues(*REST_OF_QUEUES[k + 2])
            steps(sp, body)

            def load_expert(e, par):
                if isinstance(e, int) and e >= EXPERTS:
                    return
                if not isinstance(e, int) or e >= 2:
                    sp.wait_ge(S["tags_s"], (e - 1) * 4)
                    apart(sp, "past_sp")
                chunk_done(sp, "xt2_mm", 1, e - 1, 0)
                apart(sp, "past_sp")
                start = e * QUEUE
                sp.dma_start(xs[par][:, 0:10, :],
                             queues[bass.ds(start, 10 * P), :].rearrange("(p t) c -> p t c", t=10)).then_inc(S["xs_in"], 16)
                sp.dma_start(xs[par][0:USED - 10 * P, 10, :],
                             queues[bass.ds(start + 10 * P, USED - 10 * P), :]).then_inc(S["xs_in"], 16)

            def load_weights(e, par):
                if isinstance(e, int) and e >= EXPERTS:
                    return
                if not isinstance(e, int) or e >= 2:
                    sp.wait_ge(S["w_lo"], (e - 1) * 2)
                    apart(sp, "past_sp")
                if not isinstance(e, int) or e >= 1:
                    sp.wait_ge(S["w_hi"], e * 2)
                    apart(sp, "past_sp")
                sp.dma_start(w1raw[par][:], w1[e, :, :]).then_inc(S["w_in"], 16)
                sp.dma_start(w2raw[par][:], w2[e, :, :].rearrange("(c f) h -> f c h", f=P)).then_inc(S["w_in"], 16)

            load_weights(0, 0)
            for n in range(2):
                sp.wait_ge(S[f"scattered{n}"], BATCHES // 2 * 2 * TILES * 16)
            load_expert(0, 0)

            def body2(e, par):
                load_weights(e + 1, 1 - par)
                load_expert(e + 1, 1 - par)
            experts(sp, body2)
            sp.wait_ge(S["init_out"], 16 * EXPERTS)
            sp.wait_ge(S["dump_out"], 16)
            for n in range(2):
                sp.wait_ge(S[f"base_out{n}"], 16 * BATCHES // 2)
            added_all(sp, EXPERTS)

        @block.tensor
        def _(pe):
            def mm(o, l, r, start=True, stop=True):
                return nc.tensor.matmul(o, l, r, start=start, stop=stop)

            ab, bb, cb = bank[0:2], bank[2:4], bank[4]
            m0, m1, m2 = bank[5:8]

            def readers(k, *waits):
                for name, per, batch, n in (waits if isinstance(k, int) else waits[-1:]):
                    after(pe, name, per, batch, n)

            def in_turn(n, this, before):
                return before[n:] + this[:n]

            def m0_read(k, n):
                readers(k, *in_turn(n, [("v_s", 1, k + 1, 1), ("norm_s", 2, k - 1, 1), ("roped_q", 2, k + 3, 2),
                                        ("ranked", 1, k - 2, 1)],
                                    [("v_s", 1, k, 1), ("norm_s", 2, k - 2, 1), ("roped_q", 2, k + 2, 2),
                                     ("ranked", 1, k - 3, 1)]))

            def m1_read(k, n):
                readers(k, *in_turn(n, [("mt_s", 2, k, 2), ("xct_s", 1, k + 3, 1), ("norm_s", 2, k - 1, 2),
                                        ("mt_s", 2, k + 1, 1), ("ctxt_s", 1, k - 1, 1)],
                                    [("mt_s", 2, k - 1, 2), ("xct_s", 1, k + 2, 1), ("norm_s", 2, k - 2, 2),
                                     ("mt_s", 2, k, 1), ("ctxt_s", 1, k - 2, 1)]))

            def m2_read(k, n):
                readers(k, *in_turn(n, [("xn2t_s", 1, k - 2, 1), ("indexed", 2, k - 2, 2), ("roped_k", 2, k + 3, 2),
                                        ("x1_s", 1, k - 1, 1)],
                                    [("xn2t_s", 1, k - 3, 1), ("indexed", 2, k - 3, 2), ("roped_k", 2, k + 2, 2),
                                     ("x1_s", 1, k - 2, 1)]))

            def scores_by_query(j, par, u):
                if not on(j):
                    return
                hg, i2 = divmod(u, TILES)
                if u % 4 == 0:
                    after(pe, f"packed{u // 4}", 32, j)
                after(pe, "max_s", UNITS, j, u - 1)
                for hj in range(4):
                    for odd in range(2):
                        i, h = 2 * i2 + odd, 4 * hg + hj
                        ks = max(0, BLOCK * (i - 1))
                        last = mm(ab[u % 2][BLOCK * odd:BLOCK * odd + BLOCK, hj * P:(hj + 1) * P],
                                  q_pack[par][:, h, BLOCK * i:BLOCK * (i + 1)], k_pack[par][:, odd, h, ks:ks + P])
                last.then_inc(S["a_mm"], 1)

            def scores_by_key(j, par, u):
                if not on(j):
                    return
                hg, i2 = divmod(u, TILES)
                if u % 4 == 0:
                    after(pe, f"m_packed{u // 4}", 16, j)
                after(pe, "prob_s", UNITS, j, u - 1)
                for hj in range(4):
                    for odd in range(2):
                        i, h = 2 * i2 + odd, 4 * hg + hj
                        ks = max(0, BLOCK * (i - 1))
                        last = mm(bb[u % 2][:, hj * P + odd * BLOCK:hj * P + (odd + 1) * BLOCK],
                                  k_pack[par][:, odd, h, ks:ks + P], q_pack[par][:, h, BLOCK * i:BLOCK * (i + 1)])
                last.then_inc(S["b_mm"], 1)

            def weigh_values(j, par, u):
                if not on(j):
                    return
                hg, i2 = divmod(u, TILES)
                if u == 0:
                    after(pe, "v_s", 1, j)
                if u % 4 == 0:
                    after(pe, "csb_s", 2, j, u // 4)
                after(pe, "prob_s", UNITS, j, u + 1)
                for odd in range(2):
                    i = 2 * i2 + odd
                    for hj in range(4):
                        col = (hg % 2) * TOKENS + BLOCK * i
                        last = mm(cb[32 * hj:32 * hj + 32, col:col + BLOCK],
                                  v_sb[par][:, KEY_TILE[i], 4 * hg + hj, :],
                                  probs[u % 2][:, hj * P + odd * BLOCK:hj * P + (odd + 1) * BLOCK])
                last.then_inc(S["pv_mm"], 1)

            def values(k, par):
                j = k + 1
                if on(j):
                    m0_read(k, 0)
                    after(pe, "xct_s", 1, j)
                    for a in range(3):
                        last = mm(m0[:, a * P:(a + 1) * P], xcT[1 - par][:, TOKENS + BLOCK * a:TOKENS + BLOCK * a + P],
                                  wts[:, WV:WV + DIM])
                    last.then_inc(S["v_mm"], 1)

            def maxima_across(k, j, half, n):
                if on(j):
                    m1_read(k, n)
                    after(pe, "mparts", 4, j, 2 * half + 2)
                    nc.tensor.transpose(m1[0:32, 0:64].bitcast(BF16),
                                        max_parts[half][:].rearrange("p s h i -> p (s h i)"), ident16
                                        ).then_inc(S["mt_mm"], 1)

            def inputs_across(k, par):
                j = k + 3
                if on(j):
                    m1_read(k, 1)
                    after(pe, "xn1_s", 2, j)
                    after(pe, "c_in", 16, j)
                    for t in range(TILES):
                        nc.tensor.transpose(m1[:, t * P:(t + 1) * P], xn1[1 - par][:, t, :], ident)
                    for t in range(TILES):
                        last = nc.tensor.transpose(m1[:, (2 + t) * P:(3 + t) * P], cin[1 - par][:, t, :], ident)
                    last.then_inc(S["xt_mm"], 1)

            def project(k, par, m, w, wr, cols, name, free, n):
                if on(k + 3):
                    free(k, n)
                    after(pe, "xct_s", 1, k + 3)
                    mm(m[:, 0:TOKENS], wts[:, w:w + DIM], xcT[1 - par][:, cols:cols + TOKENS])
                    mm(m[:, TOKENS:2 * TOKENS], wts[:, wr:wr + DIM], xcT[1 - par][:, cols:cols + TOKENS]
                       ).then_inc(S[name], 1)

            def context_across(k, par, t):
                j = k - 1
                if on(j):
                    (m0_read if t == 0 else m1_read)(k, 1 + t)
                    after(pe, "csb_s", 2, j)
                    for g in range(GROUPS):
                        last = nc.tensor.transpose((m0, m1)[t][:, g * P:(g + 1) * P],
                                                   csb[1 - par][:, g, t * P:(t + 1) * P], ident)
                    last.then_inc(S["ct_mm"], 1)

            def body(k, par, pair):
                if isinstance(k, int) and k == -1:
                    pe.wait_ge(S["obias_s"], 1)
                for u in range(UNITS):
                    scores_by_key(k, par, u)
                    if u < UNITS - 1:
                        scores_by_query(k + 1, 1 - par, u + 1)
                    else:
                        if isinstance(k, int) and -2 <= k < 0:
                            pe.wait_ge(S["masks_made"], 3 * (k + 3))
                        scores_by_query(k + 2, par, 0)
                    if u == 0:
                        values(k, par)
                        maxima_across(k, k, 1, 0)
                    if u == 1:
                        inputs_across(k, par)
                    if u == 2:
                        if on(k - 2):
                            m2_read(k, 0)
                            after(pe, "xn2_s", 2, k - 2)
                            for t in range(TILES):
                                last = nc.tensor.transpose(m2[:, t * P:(t + 1) * P], rows[par][:, 0, t, 0:DIM], ident)
                            last.then_inc(S["xn2t_mm"], 1)
                        context_across(k, par, 0)
                        context_across(k, par, 1)
                        if on(k - 2):
                            m2_read(k, 1)
                            for t in range(TILES):
                                last = mm(m2[:, t * EXPERTS:(t + 1) * EXPERTS], xn2T[:, t * P:(t + 1) * P],
                                          wts[:, WR:WR + EXPERTS])
                            last.then_inc(S["logit_mm"], 1)
                    if u == 3:
                        project(k, par, m0, WQ, WQR, 0, "q_mm", m0_read, 2)
                        maxima_across(k, k + 1, 0, 3)
                    if u == 4:
                        project(k, par, m2, WK, WKR, TOKENS, "k_mm", m2_read, 2)
                    if u == 5:
                        if on(k - 1):
                            m1_read(k, 4)
                            after(pe, "norm_s", 2, k - 1)
                            for t in range(TILES):
                                last = nc.tensor.transpose(m1[:, t * P:(t + 1) * P], ctxn[:, t, :], ident)
                            last.then_inc(S["ctxt_mm"], 1)
                        if on(k - 2):
                            m0_read(k, 3)
                            after(pe, "both_s", 1, k - 2)
                            b = both16[:].rearrange("p t e -> p (t e)")
                            mm(m0[:, 0:16], earlier16, b, True, False)
                            mm(m0[:, 8:16], ones16, b[:, 0:8], False, True)
                            mm(m0[:, 16:24], ones16, b[:, 0:8], True, False)
                            mm(m0[:, 16:24], ones16, b[:, 8:16], False, True).then_inc(S["prefix_mm"], 1)
                    if u == 6 and on(k - 1):
                        m2_read(k, 3)
                        after(pe, "ctxt_s", 1, k - 1)
                        for t in range(TILES):
                            last = mm(m2[:, t * P:(t + 1) * P], ctxT[:, t * P:(t + 1) * P], wts[:, WO:WO + DIM])
                        last.then_inc(S["y_mm"], 1)
                    if u == 0:
                        weigh_values(k - 1, 1 - par, UNITS - 1)
                    else:
                        weigh_values(k, par, u - 1)

            pe.wait_ge(S["consts_in"], CONST_LOADS)
            mm(cb[:, 0:DIM], cbias[:, 4:5].to_broadcast([P, P]), wts[:, WO:WO + DIM]).then_inc(S["vbias_mm"], 1)
            steps(pe, body)

            up, downs, xt, yt = bank[0:4], (bank[4], bank[7]), bank[5], bank[6]

            def rows_across(e, par, c):
                c0 = e * NCH + c
                if c == 0:
                    if isinstance(e, int) and e >= EXPERTS:
                        return
                    pe.wait_ge(S["xs_in"], e * 32 + 32)
                chunk_done(pe, "xt_hi", 1, e, c - 1)
                chunk_done(pe, "xt_lo", 1, e, c - 1)
                for t, col, n in tiles_of(c):
                    last = nc.tensor.transpose(xt[:, col:col + n], xs[par][0:n, t, 0:DIM], ident[0:n, 0:n])
                last.then_inc(S["xt2_mm"], 1)

            def hidden(e, par, c, sp_):
                n = CHUNKS[c]
                chunk_done(pe, "xt_lo", 1, e, c)
                if c == 0:
                    pe.wait_ge(S["w_lo"], 2 * e + 2)
                for f in range(FC):
                    chunk_done(pe, "h_hi", FC, e, c - 1, f + 1)
                    for i, (a, b) in enumerate(((0, 0), (1, 0), (0, 1))):
                        last = mm(up[f][:, 0:n], w1p[par][:, a, f * P:(f + 1) * P], xTp[sp_][:, b, 0:n], i == 0, i == 2)
                    last.then_inc(S["up_mm"], 1)

            def out_of_hidden(e, par, c, sp_):
                n = CHUNKS[c]
                down = downs[sp_]
                chunk_done(pe, "yt_s", 1, e, c - 2)
                for f in range(FC):
                    chunk_done(pe, "h_lo", FC, e, c, f + 1)
                    for i, (a, b) in enumerate(((0, 0), (1, 0), (0, 1))):
                        last = mm(down[:, 0:n], w2p[par][:, a, f, :], hidp[sp_][:, b, f, 0:n],
                                  f == 0 and i == 0, f == FC - 1 and i == 2)
                last.then_inc(S["down_mm"], 1)

            def results_across(e, c, sp_):
                chunk_done(pe, "yt_s", 1, e, c)
                chunk_done(pe, "ys_s", 1, e, c - 1)
                for t, col, n in tiles_of(c):
                    last = nc.tensor.transpose(yt[0:n, (col // P) * DIM:(col // P + 1) * DIM], yT[sp_][:, col:col + n], ident)
                last.then_inc(S["yt_mm"], 1)

            def body2(e, par):
                first = isinstance(e, int) and e == 0
                for c in range(NCH):
                    s = (e_par(par) + c) % 2
                    hidden(e, par, c, s)
                    if c < NCH - 1:
                        rows_across(e, par, c + 1)
                    else:
                        rows_across(e + 1, 1 - par, 0)
                    if c >= 1:
                        out_of_hidden(e, par, c - 1, 1 - s)
                    elif not first:
                        out_of_hidden(e - 1, 1 - par, NCH - 1, 1 - s)
                    if c >= 2:
                        results_across(e, c - 2, s)
                    elif not first:
                        results_across(e - 1, c + 1, s)

            def e_par(par):
                return par * NCH

            rows_across(0, 0, 0)
            experts(pe, body2)
            e = EXPERTS - 1
            s = (NCH * EXPERTS - 1) % 2
            out_of_hidden(e, e % 2, NCH - 1, s)
            results_across(e, NCH - 2, 1 - s)
            results_across(e, NCH - 1, s)

        @block.scalar
        def _(act):
            bb, cb = bank[2:4], bank[4]
            m0, m1, m2 = bank[5:8]

            def exponentials(k, par, u):
                if not on(k):
                    return
                after(act, "b_mm", UNITS, k, u + 1)
                after(act, "pv_mm", UNITS, k, u - 1)
                nc.scalar.activation(probs[u % 2][:], bb[u % 2][:], ACT.Exp).then_inc(S["prob_s"], 1)

            def copy_sums(j, par, p):
                if not on(j):
                    return
                after(act, "pv_mm", UNITS, j, 4 * p + 4)
                after(act, "ct_mm", 2, j - 2)
                nc.scalar.copy(csb[par][:, 2 * p:2 * p + 2, :].rearrange("p g t -> p (g t)"), cb[:]).then_inc(S["csb_s"], 1)

            def copy_maxima(j, half):
                if not on(j):
                    return
                after(act, "mt_mm", 2, j, half + 1)
                after(act, "mscr_w", 32, j - 1, 16 * half + 16)
                nc.scalar.copy(maxT[half][:], m1[0:32, 0:64].bitcast(BF16)).then_inc(S["mt_s"], 1)

            def body(k, par, pair):
                copy_maxima(k, 1)
                exponentials(k, par, 0)
                if isinstance(k, int) and k == -1:
                    act.wait_ge(S["v_ones"], 4)
                if on(k + 1):
                    after(act, "v_mm", 1, k + 1)
                    after(act, "pv_mm", UNITS, k - 1)
                    nc.scalar.copy(v_sb[1 - par][:, :, :, 0:HD],
                                   m0[:, 0:3 * P].rearrange("p (a h c) -> p a h c", a=3, c=HD)).then_inc(S["v_s"], 1)
                copy_sums(k - 1, 1 - par, 1)
                exponentials(k, par, 1)
                if on(k + 3):
                    after(act, "xt_mm", 1, k + 3)
                    after(act, "v_mm", 1, k + 1)
                    nc.scalar.copy(xcT[1 - par][:], m1[:]).then_inc(S["xct_s"], 1)
                exponentials(k, par, 2)
                if on(k - 2):
                    after(act, "xn2t_mm", 1, k - 2)
                    after(act, "logit_mm", 1, k - 3)
                    nc.scalar.copy(xn2T[:], m2[:, 0:TOKENS]).then_inc(S["xn2t_s"], 1)
                if on(k - 2):
                    after(act, "xn2_s", 2, k - 2)
                    nc.scalar.copy(rows[par][:, 1, :, 0:DIM], rows[par][:, 0, :, 0:DIM]).then_inc(S["rowcopy_s"], 1)
                exponentials(k, par, 3)
                copy_maxima(k + 1, 0)
                exponentials(k, par, 4)
                copy_sums(k, par, 0)
                if on(k - 2):
                    after(act, "top_s", 1, k - 2)
                    nc.scalar.activation(ediff[:], diff[:], ACT.Exp).then_inc(S["exp_gate"], 1)
                exponentials(k, par, 5)
                if on(k - 1):
                    after(act, "ctxt_mm", 1, k - 1)
                    after(act, "y_mm", 1, k - 2)
                    nc.scalar.copy(ctxT[:], m1[:, 0:TOKENS]).then_inc(S["ctxt_s"], 1)
                exponentials(k, par, 6)
                if on(k + 3):
                    after(act, "qk_s", 1, k + 3)
                    after(act, "scr_w", 96, k + 2)
                    nc.scalar.copy(parts[:, 0, :, :], qk[:]).then_inc(S["part1"], 1)
                exponentials(k, par, 7)
                if on(k + 3):
                    after(act, "rest_s", 1, k + 3)
                    nc.scalar.copy(parts[:, 1, :, :], rest[:]).then_inc(S["part2"], 1)

            steps(act, body)

            up, downs, xt = bank[0:4], (bank[4], bank[7]), bank[5]

            def split_rows(e, c, s):
                if isinstance(e, int) and e >= EXPERTS:
                    return
                chunk_done(act, "xt2_mm", 1, e, c)
                chunk_done(act, "up_mm", FC, e, c - 2)
                nc.scalar.copy(xTp[s][:, 0, 0:CHUNKS[c]], xt[:, 0:CHUNKS[c]]).then_inc(S["xt_hi"], 1)

            def split_weights(e, par):
                if isinstance(e, int) and e >= EXPERTS:
                    return
                act.wait_ge(S["w_in"], 32 * e + 32)
                chunk_done(act, "down_mm", 1, e - 2, NCH - 1)
                nc.scalar.copy(w1p[par][:, 0, :], w1raw[par][:]).then_inc(S["w_hi"], 1)
                nc.scalar.copy(w2p[par][:, 0, :, :], w2raw[par][:]).then_inc(S["w_hi"], 1)

            def copy_results(e, c, s):
                chunk_done(act, "down_mm", 1, e, c)
                chunk_done(act, "yt_mm", 1, e, c - 2)
                nc.scalar.copy(yT[s][:, 0:CHUNKS[c]], downs[s][:, 0:CHUNKS[c]]).then_inc(S["yt_s"], 1)

            split_weights(0, 0)
            split_rows(0, 0, 0)

            def body2(e, par):
                first = isinstance(e, int) and e == 0
                for c in range(NCH):
                    s = (par * NCH + c) % 2
                    for f in range(FC):
                        if f == 2:
                            if c < NCH - 1:
                                split_rows(e, c + 1, 1 - s)
                            else:
                                split_rows(e + 1, 0, 1 - s)
                        chunk_done(act, "up_mm", FC, e, c, f + 1)
                        chunk_done(act, "h_lo", FC, e, c - 2, f + 1)
                        nc.scalar.activation(hid[s][:, f, 0:CHUNKS[c]], up[f][:, 0:CHUNKS[c]], ACT.Silu
                                             ).then_inc(S["silu_s"], 1)
                        if f == 0:
                            chunk_done(act, "down_mm", 1, e, c - 2)
                        nc.scalar.activation(hidp[s][:, 0, f, 0:CHUNKS[c]], up[f][:, 0:CHUNKS[c]], ACT.Silu
                                             ).then_inc(S["h_hi"], 1)
                    if c >= 1:
                        copy_results(e, c - 1, 1 - s)
                    elif not first:
                        copy_results(e - 1, NCH - 1, 1 - s)
                    if c == 0:
                        split_weights(e + 1, 1 - par)
            experts(act, body2)
            copy_results(EXPERTS - 1, NCH - 1, (NCH * EXPERTS - 1) % 2)

        @block.vector
        def _(dve):
            v = nc.vector
            ab, m0, m1, m2 = bank[0:2], bank[5], bank[6], bank[7]
            cb = bank[4]

            def maximum(j, par, u):
                if not on(j):
                    return
                hg, i2 = divmod(u, TILES)
                after(dve, "a_mm", UNITS, j, u + 1)
                if u == 0:
                    after(dve, "mparts", 4, j - 2)
                v.reduce_max(maxima[par][:, 4 * hg:4 * hg + 4, i2],
                             ab[u % 2][:].rearrange("p (h c) -> p h c", c=P), AX).then_inc(S["max_s"], 1)

            def maximum_parts(j, par, half, n):
                if not on(j):
                    return
                src = maxima[par][:, 8 * half:8 * half + 8, :]
                if n == 0:
                    after(dve, "max_s", UNITS, j, 4 * half + 4)
                    after(dve, "mt_mm", 2, j - 1, half + 1)
                    v.tensor_scalar(max_parts[half][:, 0, :, :], src, -1.0, None, ALU.mult).then_inc(S["mparts"], 1)
                else:
                    after(dve, "mparts", 4, j, 2 * half + 1)
                    v.scalar_tensor_tensor(max_parts[half][:, 1, :, :], src, -1.0, max_parts[half][:, 0, :, :],
                                           ALU.mult, ALU.subtract).then_inc(S["mparts"], 1)

            def norm1(k, par, n):
                j = k + 4
                if not on(j):
                    return
                if n == 0:
                    after(dve, "x_in", 16, j)
                    after(dve, "mv1_s", 2, j - 1)
                    for t in range(TILES):
                        v.bn_stats(stats1[:, t, :], xin[par][:, t, :]).then_inc(S["stats1_s"], 1)
                elif n == 1:
                    after(dve, "stats1_s", 2, j)
                    apart(dve, "past_dve")
                    after(dve, "xn1_s", 2, j - 1)
                    apart(dve, "past_dve")
                    for t in range(TILES):
                        v.bn_aggr(mv1[:, t, :], stats1[:, t, :]).then_inc(S["mv1_s"], 1)
                elif n == 2:
                    after(dve, "mv1_s", 2, j)
                    after(dve, "rstd1_s", 1, j - 1)
                    v.tensor_scalar(var1[:], mv1[:, :, 1], EPS, None, ALU.add).then_inc(S["var1_s"], 1)
                else:
                    after(dve, "rstd1_s", 1, j)
                    after(dve, "xt_mm", 1, j - 2)
                    for t in range(TILES):
                        v.tensor_scalar(xn1[par][:, t, :], xin[par][:, t, :], mv1[:, t, 0:1], rstd1[:, t:t + 1],
                                        ALU.subtract, ALU.mult).then_inc(S["xn1_s"], 1)

            def norm2(k, par, n):
                j = k - 1
                if not on(j):
                    return
                if n == 0:
                    after(dve, "x1_s", 1, j)
                    after(dve, "mv2_s", 2, j - 1)
                    for t in range(TILES):
                        v.bn_stats(stats2[:, t, :], x1[1 - par][:, t, :]).then_inc(S["stats2_s"], 1)
                elif n == 1:
                    after(dve, "stats2_s", 2, j)
                    apart(dve, "past_dve")
                    after(dve, "xn2_s", 2, j - 1)
                    apart(dve, "past_dve")
                    for t in range(TILES):
                        v.bn_aggr(mv2[:, t, :], stats2[:, t, :]).then_inc(S["mv2_s"], 1)
                else:
                    after(dve, "mv2_s", 2, j)
                    after(dve, "rstd2_s", 1, j - 1)
                    v.tensor_scalar(var2[:], mv2[:, :, 1], EPS, None, ALU.add).then_inc(S["var2_s"], 1)

            def normalise_result(k, par, pair, t):
                j = k - 2
                if not on(j):
                    return
                if t == 0:
                    after(dve, "rstd2_s", 1, j)
                    after_same(dve, "scattered", 64, par, pair, -4)
                    after_same(dve, "base_out", 16, par, pair, -4)
                v.tensor_scalar(rows[par][:, 0, t, 0:DIM], x1[par][:, t, :], mv2[:, t, 0:1], rstd2[:, t:t + 1],
                                ALU.subtract, ALU.mult).then_inc(S["xn2_s"], 1)

            def context(k):
                j = k - 1
                if not on(j):
                    return
                sums = [m[:].rearrange("p (h c) -> p h c", c=32) for m in (m0, m1)]
                for t in range(TILES):
                    after(dve, "ct_mm", 2, j, t + 1)
                    if t == 0:
                        after(dve, "norm_s", 2, j - 1)
                    v.reciprocal(recip[t][:], sums[t][:, :, HD]).then_inc(S["rec_s"], 1)
                after(dve, "ctxt_mm", 1, j - 1)
                for t in range(TILES):
                    after(dve, "rec_s", 2, j, t + 1)
                    v.tensor_tensor(ctxn[:, t, :].rearrange("p (h c) -> p h c", c=HD), sums[t][:, :, 0:HD],
                                    recip[t][:].unsqueeze(2).to_broadcast([P, HEADS, HD]), ALU.mult
                                    ).then_inc(S["norm_s"], 1)

            def rope(k, name, mms, m, which, c0, b0, i):
                if not on(k + 3):
                    return
                if i == 0:
                    after(dve, mms, 1, k + 3)
                    after(dve, "qk_s", 1, k + 2)
                v.scalar_tensor_tensor((straight, turned)[i][:, which, :], m[:, i * TOKENS:(i + 1) * TOKENS],
                                       cbias[:, b0 + i:b0 + i + 1], cst[:, c0 + i * TOKENS:c0 + (i + 1) * TOKENS],
                                       ALU.add, ALU.mult).then_inc(S[name], 1)

            def route(k, par, n):
                j = k - 2
                if not on(j):
                    return

                def done(ins):
                    ins.then_inc(S["router"], 1)

                def need(count):
                    after(dve, "router", ROUTER, j, count)
                if n == 0:
                    after(dve, "gate_s", 3, j - 1)
                    apart(dve, "past_dve")
                    after(dve, "logit_mm", 1, j)
                    apart(dve, "past_dve")
                    for t in range(TILES):
                        done(v.max(top[:, t, :], m2[:, t * EXPERTS:(t + 1) * EXPERTS]))
                elif n == 1:
                    need(2)
                    apart(dve, "past_dve")
                    for t in range(TILES):
                        v.max_index(top_index[:, t, :], top[:, t, :], m2[:, t * EXPERTS:(t + 1) * EXPERTS]
                                    ).then_inc(S["indexed"], 1)
                elif n == 2:
                    v.tensor_tensor(diff[:], top[:, :, 1], top[:, :, 0], ALU.subtract).then_inc(S["top_s"], 1)
                    after(dve, "indexed", 2, j)
                    done(v.tensor_tensor(chosen[:],
                                         cst[:, EXPERT:EXPERT + 8].unsqueeze(1).unsqueeze(1).to_broadcast([P, 2, TILES, 8]),
                                         top_index[:, :, 0:2].rearrange("p t s -> p s t").unsqueeze(3).to_broadcast(
                                             [P, 2, TILES, 8]), ALU.is_equal))
                elif n == 3:
                    need(3)
                    after(dve, "prefix_mm", 1, j - 1)
                    v.tensor_tensor(both16[:], chosen[:, 0, :, :], chosen[:, 1, :, :], ALU.add).then_inc(S["both_s"], 1)
                elif n == 4:
                    after(dve, "prefix_mm", 1, j)
                    dve.wait_ge(S["counted"], 1)
                    after(dve, "ranked", 1, j - 1)
                    done(v.tensor_tensor(place[:], m0[:, 0:16].rearrange("p (t e) -> p t e", t=TILES),
                                         count[:].unsqueeze(1).to_broadcast([P, TILES, EXPERTS]), ALU.add))
                    after(dve, "exp_gate", 1, j)
                    done(v.tensor_scalar(gate[:, 0, :], ediff[:], 1.0, None, ALU.add))
                    need(4)
                    done(v.tensor_tensor(over[:], place[:], cst[:, LIMIT:LIMIT + 8].unsqueeze(1).to_broadcast(
                        [P, TILES, EXPERTS]), ALU.is_ge))
                    v.tensor_tensor(count[:], count[:], m0[:, 16:24], ALU.add).then_inc(S["ranked"], 1)
                elif n == 5:
                    need(6)
                    done(v.scalar_tensor_tensor(place2[:], over[:], FAR, place[:], ALU.mult, ALU.add))
                    need(5)
                    done(v.reciprocal(gate[:, 1, :], gate[:, 0, :]))
                elif n == 6:
                    need(7)
                    done(v.tensor_tensor(picked[:], chosen[:], place2[:].unsqueeze(1).to_broadcast(
                        [P, 2, TILES, EXPERTS]), ALU.mult))
                    need(8)
                    v.tensor_copy(rows[par][:, 0, :, DIM], gate[:, 1, :]).then_inc(S["gate_s"], 1)
                    v.tensor_tensor(rows[par][:, 1, :, DIM], gate[:, 1, :], ediff[:], ALU.mult).then_inc(S["gate_s"], 1)
                else:
                    need(9)
                    with nc.allow_low_precision(reason="places are whole numbers below 2**24"):
                        v.reduce_sum(index[par][:], picked[:].rearrange("p s t e -> p (s t) e"), AX
                                     ).then_inc(S["gate_s"], 1)

            def masks(n):
                if n == 0:
                    dve.wait_ge(S["masks_in"], 32)
                for dst, src in ((q_pack[n], 0), (k_pack[n][:, 0], 1), (k_pack[n][:, 1], 2)):
                    v.tensor_copy(dst[MASK_ROW:P], mask_rows[MASK_ROW:P, src, :].unsqueeze(1).to_broadcast(
                        [P - MASK_ROW, HEADS, TOKENS])).then_inc(S["masks_made"], 1)

            def start():
                dve.wait_ge(S["vbias_mm"], 1)
                v.tensor_tensor(rbias[:], rbias[:], cb[:, 0:DIM], ALU.add).then_inc(S["obias_s"], 1)

            def body(k, par, pair):
                other = 1 - par
                maximum(k + 1, other, 1)
                norm1(k, par, 0)
                normalise_result(k, par, pair, 0)
                normalise_result(k, par, pair, 1)
                maximum(k + 1, other, 2)
                norm1(k, par, 1)
                maximum(k + 1, other, 3)
                context(k)
                maximum_parts(k + 1, other, 0, 0)
                norm1(k, par, 2)
                maximum_parts(k + 1, other, 0, 1)
                route(k, par, 0)
                maximum(k + 1, other, 4)
                route(k, par, 1)
                rope(k, "roped_q", "q_mm", m0, 0, COSQ, 0, 0)
                route(k, par, 2)
                rope(k, "roped_q", "q_mm", m0, 0, COSQ, 0, 1)
                route(k, par, 3)
                maximum(k + 1, other, 5)
                norm1(k, par, 3)
                if isinstance(k, int) and k == FIRST:
                    start()
                rope(k, "roped_k", "k_mm", m2, 1, COSK, 2, 0)
                rope(k, "roped_k", "k_mm", m2, 1, COSK, 2, 1)
                if isinstance(k, int) and -3 <= k < -1:
                    masks(k + 3)
                maximum(k + 1, other, 6)
                route(k, par, 4)
                route(k, par, 5)
                route(k, par, 6)
                maximum(k + 1, other, 7)
                route(k, par, 7)
                maximum_parts(k + 1, other, 1, 0)
                if on(k - 1):
                    after(dve, "y_mm", 1, k - 1)
                    after(dve, "xrb_s", 1, k - 1)
                    after(dve, "base_s", 1, k - 3)
                    v.tensor_tensor(x1[other][:].rearrange("p t c -> p (t c)"),
                                    xres[other][:].rearrange("p t c -> p (t c)"), m2[:, 0:TOKENS], ALU.add
                                    ).then_inc(S["x1_s"], 1)
                maximum_parts(k + 1, other, 1, 1)
                norm2(k, par, 0)
                maximum(k + 2, par, 0)
                norm2(k, par, 1)
                norm2(k, par, 2)
            steps(dve, body)

            xt, yt = bank[5], bank[6]

            def rest_of_rows(e, c, s):
                if isinstance(e, int) and e >= EXPERTS:
                    return
                chunk_done(dve, "xt_hi", 1, e, c)
                v.tensor_tensor(xTp[s][:, 1, 0:CHUNKS[c]], xt[:, 0:CHUNKS[c]], xTp[s][:, 0, 0:CHUNKS[c]].bitcast(F32),
                                ALU.subtract).then_inc(S["xt_lo"], 1)

            def rest_of_weights(e, par):
                if isinstance(e, int) and e >= EXPERTS:
                    return
                dve.wait_ge(S["w_hi"], 2 * e + 2)
                v.tensor_tensor(w1p[par][:, 1, :], w1raw[par][:], w1p[par][:, 0, :].bitcast(F32), ALU.subtract
                                ).then_inc(S["w_lo"], 1)
                v.tensor_tensor(w2p[par][:, 1, :, :], w2raw[par][:], w2p[par][:, 0, :, :].bitcast(F32), ALU.subtract
                                ).then_inc(S["w_lo"], 1)

            def weigh_results(e, par, c, s):
                chunk_done(dve, "yt_mm", 1, e, c)
                if isinstance(e, int) or c == 0:
                    dve.wait_ge(S["tags_s"], 4 * e + 4)
                back, since = (c - 2) % NCH, e if c >= 2 else e - 1
                if not isinstance(e, int) or since >= 0:
                    each = 16 * len(tiles_of(back))
                    dve.wait_ge(S[f"added{back}"], since * each + each)
                full = [t for t in tiles_of(c) if t[2] == P]
                part = [t for t in tiles_of(c) if t[2] < P]
                t0, m = full[0][0], len(full)
                ins = v.tensor_tensor(ys[s][:, 0:m, :], yt[:, 0:m * DIM].rearrange("p (t c) -> p t c", c=DIM),
                                      row_gate[par][:, t0:t0 + m].unsqueeze(2).to_broadcast([P, m, DIM]), ALU.mult)
                for t, col, n in part:
                    i = col // P
                    ins = v.tensor_tensor(ys[s][0:n, i, :], yt[0:n, i * DIM:(i + 1) * DIM],
                                          row_gate[par][0:n, t:t + 1].to_broadcast([n, DIM]), ALU.mult)
                ins.then_inc(S["ys_s"], 1)

            rest_of_weights(0, 0)
            rest_of_rows(0, 0, 0)

            def body2(e, par):
                first = isinstance(e, int) and e == 0
                for c in range(NCH):
                    s = (par * NCH + c) % 2
                    for f in range(FC):
                        if f == 2:
                            if c < NCH - 1:
                                rest_of_rows(e, c + 1, 1 - s)
                            else:
                                rest_of_rows(e + 1, 0, 1 - s)
                        chunk_done(dve, "silu_s", FC, e, c, f + 1)
                        chunk_done(dve, "h_hi", FC, e, c, f + 1)
                        v.tensor_tensor(hidp[s][:, 1, f, 0:CHUNKS[c]], hid[s][:, f, 0:CHUNKS[c]],
                                        hidp[s][:, 0, f, 0:CHUNKS[c]].bitcast(F32), ALU.subtract
                                        ).then_inc(S["h_lo"], 1)
                    if c >= 2:
                        weigh_results(e, par, c - 2, s)
                    elif not first:
                        weigh_results(e - 1, 1 - par, c + 1, s)
                    if c == 0:
                        rest_of_weights(e + 1, 1 - par)
            experts(dve, body2)
            e = EXPERTS - 1
            s = (NCH * EXPERTS - 1) % 2
            weigh_results(e, e % 2, NCH - 2, 1 - s)
            weigh_results(e, e % 2, NCH - 1, s)

        @block.gpsimd
        def _(pool):
            g = nc.gpsimd
            g.memset(half_neg[:], -0.5).then_inc(S["half_set"], 1)
            g.memset(empty[:], 0.0).then_inc(S["init_made"], 1)
            pool.wait_ge(S["init_made"], 1)
            g.iota(empty[:, :, DIM + 1].bitcast(I32), pattern=[[1, INIT_R]], base=ALL, channel_multiplier=INIT_R
                   ).then_inc(S["init_made"], 1)
            pool.wait_ge(S["half_set"], 1)

            def rows_out(k, par):
                j = k - 2
                if not on(j):
                    return
                pool.wait_ge(S["init_out"], 16 * EXPERTS)
                after(pool, "gate_s", 3, j)
                after(pool, "rowcopy_s", 1, j)
                after(pool, "tok_s", 2, j)
                apart(pool, "past_pool")
                for n in range(2 * TILES):
                    g.indirect_dma_start(queues, bass.IndirectOffsetOnAxis(ap=index[par][:, n:n + 1], axis=0),
                                         rows[par][:, n // TILES, n % TILES, :], None,
                                         bounds_check=EXPERTS * QUEUE - 1, oob_is_err=False).then_inc(S[f"scattered{par}"], 16)

            def start():
                for n in range(2):
                    g.memset(v_sb[n][:], 0.0).then_inc(S["v_ones"], 1)
                pool.wait_ge(S["v_ones"], 2)
                for n in range(2):
                    g.memset(v_sb[n][:, :, :, HD:2 * HD], 1.0).then_inc(S["v_ones"], 1)
                pool.wait_ge(S["consts_in"], CONST_LOADS)
                g.tensor_copy(count[:], cst[:, START:START + 8]).then_inc(S["counted"], 1)
                g.tensor_copy(tok[:], cst[:, TOK:TOK + 2]).then_inc(S["half_set"], 1)
                pool.wait_ge(S["half_set"], 2)

            def body(k, par, pair):
                if on(k - 2):
                    j = k - 2
                    after(pool, "xn2_s", 2, j)
                    apart(pool, "past_pool")
                    g.tensor_tensor(base[par][:], x1[par][:], rows[par][:, 0, :, 0:DIM], ALU.add).then_inc(S["base_s"], 1)
                    after(pool, "tok_s", 2, j - 1)
                    apart(pool, "past_pool")
                    g.tensor_copy(rows[par][:, :, :, DIM + 1].bitcast(I32),
                                  tok[:].unsqueeze(1).to_broadcast([P, 2, TILES])).then_inc(S["tok_s"], 1)
                    after(pool, "tok_s", 2, j, 1)
                    apart(pool, "past_pool")
                    g.tensor_scalar(tok[:], tok[:], float(TOKENS), None, ALU.add).then_inc(S["tok_s"], 1)
                if on(k + 4):
                    after(pool, "var1_s", 1, k + 4)
                    after(pool, "xn1_s", 2, k + 3)
                    g.tensor_tensor(rstd1[:], var1[:], half_neg[:], ALU.pow).then_inc(S["rstd1_s"], 1)
                if on(k - 1):
                    after(pool, "xr_in", 16, k - 1)
                    pool.wait_ge(S["obias_s"], 1)
                    g.tensor_tensor(xres[1 - par][:], xres[1 - par][:],
                                    rbias[:].unsqueeze(1).to_broadcast([P, TILES, DIM]), ALU.add
                                    ).then_inc(S["xrb_s"], 1)
                if isinstance(k, int) and k == FIRST:
                    start()
                if on(k + 3):
                    after(pool, "roped_q", 2, k + 3)
                    after(pool, "roped_k", 2, k + 3)
                    after(pool, "part1", 1, k + 2)
                    after(pool, "rest_s", 1, k + 2)
                    g.tensor_tensor(qk[:], straight[:], turned[:], ALU.add).then_inc(S["qk_s"], 1)
                    after(pool, "part1", 1, k + 3)
                    after(pool, "part2", 1, k + 2)
                    g.tensor_tensor(rest[:], qk[:], parts[:, 0, :, :], ALU.subtract).then_inc(S["rest_s"], 1)
                if on(k + 3):
                    after(pool, "part2", 1, k + 3)
                    g.tensor_tensor(parts[:, 2, :, :], rest[:], parts[:, 1, :, :], ALU.subtract).then_inc(S["part3"], 1)
                if on(k - 1):
                    after(pool, "var2_s", 1, k - 1)
                    after(pool, "xn2_s", 2, k - 2)
                    g.tensor_tensor(rstd2[:], var2[:], half_neg[:], ALU.pow).then_inc(S["rstd2_s"], 1)
                rows_out(k, par)
            steps(pool, body)

            for n in range(2):
                pool.wait_ge(S[f"base_out{n}"], 16 * BATCHES // 2)
            pool.wait_ge(S["dump_out"], 16)

            def body2(e, par):
                pool.wait_ge(S["xs_in"], e * 32 + 32)
                if not isinstance(e, int) or e > 0:
                    added_all(pool, e - 1)
                apart(pool, "past_pool")
                for n, a, b in ((P, 0, 10), (USED - 10 * P, 10, 11)):
                    g.tensor_copy(row_gate[par][0:n, a:b], xs[par][0:n, a:b, DIM]).then_inc(S["tags_s"], 1)
                    g.tensor_copy(row_token[par][0:n, a:b], xs[par][0:n, a:b, DIM + 1].bitcast(I32)
                                  ).then_inc(S["tags_s"], 1)
                for c in range(NCH):
                    s = (par * NCH + c) % 2
                    chunk_done(pool, "ys_s", 1, e, c)
                    if c == 0:
                        pool.wait_ge(S["tags_s"], 4 * e + 4)
                    if c == 0 and (not isinstance(e, int) or e > 0):
                        added_all(pool, e)
                    apart(pool, "past_pool")
                    for t, col, n in tiles_of(c):
                        g.indirect_dma_start(out, bass.IndirectOffsetOnAxis(
                            ap=row_token[par][0:n, t:t + 1], axis=0),
                            ys[s][0:n, col // P, :], None, compute_op=ALU.add).then_inc(S[f"added{c}"], 16)
            experts(pool, body2)
            added_all(pool, EXPERTS)


def shape_constants():
    f = np.float32
    c = np.zeros((P, CONSTS), f)
    c[:, IDENT:IDENT + P] = np.eye(P, dtype=f)
    half = HD // 2
    freqs = (f(1.0) / f(10000.0) ** (np.arange(half, dtype=f) / f(half))).astype(f)
    ang = np.arange(TOKENS, dtype=f)[None, :] * freqs[(np.arange(P) // HEADS) % half][:, None]
    cos, sin = np.cos(ang).astype(f), np.sin(ang).astype(f)
    sin = np.where((np.arange(P) // HEADS < half)[:, None], -sin, sin)
    scale = f(HD ** -0.5)
    c[:, COSQ:COSQ + TOKENS], c[:, SINQ:SINQ + TOKENS] = cos * scale, sin * scale
    c[:, COSK:COSK + TOKENS], c[:, SINK:SINK + TOKENS] = cos, sin
    e = np.arange(EXPERTS)
    c[:, EXPERT:EXPERT + 8] = e
    c[:, LIMIT:LIMIT + 8] = e * QUEUE + CAPACITY
    c[:, START:START + 8] = e * QUEUE
    c[:, TOK:TOK + 2] = np.arange(P)[:, None] + np.arange(TILES) * P
    c16 = np.zeros((P, 3 * P), f)
    c16[:, 0:P] = np.eye(P)
    c16[:, P:2 * P] = np.triu(np.ones((P, P)), 1)
    c16[:, 2 * P:] = 1
    t = np.arange(TOKENS)
    q = np.zeros((CONST_ROWS, TOKENS), f)
    q[0] = t < BLOCK
    q[MASK_ROW - FLAG_ROW:] = (t % BLOCK)[None, :] == np.arange(BLOCK)[:, None]
    k = np.zeros((CONST_ROWS, 2, TOKENS), f)
    k[0] = np.where(t // BLOCK == 1, MASKED, 0)
    k[1:3] = 1
    j, r = np.arange(BLOCK)[:, None], (t % BLOCK)[None, :]
    for odd in range(2):
        under = (t // BLOCK % 2 == odd)[None, :]
        k[MASK_ROW - FLAG_ROW:, odd] = np.where(np.where(under, r <= j, r >= j), 0, MASKED)
    b = mybir.dt.np(BF16)
    return c, c16.astype(b), q.astype(b), k.astype(b)


def kernel(x, ctx_1024, L0_xattn_q_w, L0_xattn_q_b, L0_xattn_k_w, L0_xattn_k_b, L0_xattn_v_w, L0_xattn_v_b,
           L0_xattn_o_w, L0_xattn_o_b, L0_ffn_router_w, L0_ffn_w1, L0_ffn_w2):
    import concourse.bacc as bacc
    from concourse.bass_utils import run_bass_kernel_spmd

    def by_dim(w, turn):
        a = np.asarray(w).reshape((HEADS, HD) + np.asarray(w).shape[1:])
        if turn:
            a = np.concatenate([a[:, HD // 2:], a[:, :HD // 2]], axis=1)
        a = np.swapaxes(a, 0, 1)
        return a.reshape((DIM,) + a.shape[2:])

    qw, kw = np.asarray(L0_xattn_q_w), np.asarray(L0_xattn_k_w)
    weights = np.concatenate([by_dim(qw, False).T, by_dim(qw, True).T, by_dim(kw, False).T, by_dim(kw, True).T,
                              np.asarray(L0_xattn_v_w).T, np.asarray(L0_xattn_o_w).T,
                              np.asarray(L0_ffn_router_w).T], axis=1)
    qb, kb = np.asarray(L0_xattn_q_b), np.asarray(L0_xattn_k_b)
    col_bias = np.stack([by_dim(qb, False), by_dim(qb, True), by_dim(kb, False), by_dim(kb, True),
                         np.asarray(L0_xattn_v_b)], axis=1)
    row_bias = np.asarray(L0_xattn_o_b)
    c, c16, q_rows, k_rows = shape_constants()
    arrays = {"x": x, "ctx": ctx_1024, "weights": weights, "col_bias": col_bias, "row_bias": row_bias,
              "consts": c, "consts16": c16, "q_rows": q_rows, "k_rows": k_rows, "w1": L0_ffn_w1, "w2": L0_ffn_w2}
    arrays = {f"in_{n}": np.ascontiguousarray(a) for n, a in arrays.items()}
    nc = bacc.Bacc("TRN2", target_bir_lowering=False, num_devices=1)
    ins = [nc.dram_tensor(n, a.shape, mybir.dt.from_np(a.dtype), kind="ExternalInput").ap() for n, a in arrays.items()]
    out = nc.dram_tensor("out", [ALL + QUEUE, DIM], F32, kind="ExternalOutput").ap()
    build(nc, *ins, out)
    r = run_bass_kernel_spmd(nc, [arrays], core_ids=[0])
    return r.results[0]["out"][:ALL].reshape(BATCHES, TOKENS, DIM)
```
